# Optimizing a Trainium2 kernel written in Bass

```python
import numpy as np
import jax
import jax.numpy as jnp

def _softmax(x, axis=-1):
    return jax.nn.softmax(x, axis=axis)

def _gelu(x):
    return jax.nn.gelu(x, approximate=True)

def _silu(x):
    return jax.nn.silu(x)

def _sigmoid(x):
    return jax.nn.sigmoid(x)

def _layernorm(x, axis=-1, eps=1e-05):
    m = jnp.mean(x, axis=axis, keepdims=True)
    v = jnp.var(x, axis=axis, keepdims=True)
    return (x - m) / jnp.sqrt(v + eps)

def _scatter_add(tgt, idx, src, axis=0):
    return tgt.at[idx].add(src)

def _segment_sum(src, seg, n):
    return jax.ops.segment_sum(src, seg, n)
kernel_name = 'mk_adaln_attn_ffn_d1_seqx_r8_36679a'

def setup_inputs(seed: int=0):
    np.random.seed(seed)
    _w = jnp.asarray

    def _rec_inputs():
        import jax
        import jax.numpy as jnp
        _rk = jax.random.key(seed)
        x = -0.000125 + 0.9999 * jax.random.normal(jax.random.fold_in(_rk, 1), (16, 128, 128), jnp.float32)
        _lenS = 128 - jax.random.randint(jax.random.fold_in(_rk, 7), (16,), 0, max(1, 128 // 4) + 1, jnp.int32)
        _lenS2 = 128 - jax.random.randint(jax.random.fold_in(_rk, 8), (16,), 0, max(1, 128 // 4) + 1, jnp.int32)
        cond_1024 = -0.00493535 + 1.00056 * jax.random.normal(jax.random.fold_in(_rk, 11), (16, 128), jnp.float32)
        return (x, cond_1024)
    x, cond_1024 = _rec_inputs()

    def _L0_cond_setup():
        import jax, jax.numpy as jnp
        import numpy as np
        import math
        N, T, D, H = (64, 64, 128, 128)
        key = jax.random.key(seed)
        k1, k2, k3, k4 = jax.random.split(key, 4)
        x = jax.random.normal(k1, (N, T, D), dtype=jnp.float32)
        h0 = jax.random.normal(k2, (N, H), dtype=jnp.float32)
        Wx = jax.random.normal(k3, (D, 4 * H), dtype=jnp.float32) / math.sqrt(D)
        Wh = jax.random.normal(k4, (H, 4 * H), dtype=jnp.float32) / math.sqrt(H)
        b = jnp.zeros((4 * H,), dtype=jnp.float32)
        return {'x': x, 'h0': h0, 'Wx': Wx, 'Wh': Wh, 'b': b}
    _L0_cond_all = _L0_cond_setup()
    _L0_cond_in = {k: v for k, v in _L0_cond_all.items() if k in ('Wx', 'Wh', 'b')}
    del _L0_cond_all

    def _L0_attn_setup():
        import jax, jax.numpy as jnp
        import numpy as np
        B, L, D = (2, 256, 128)
        H, HD = (16, 64)
        LD = 32
        key = jax.random.key(seed)
        ks = jax.random.split(key, 6)
        s = lambda fan_in: 1.0 / np.sqrt(fan_in)
        x_bld = jax.random.normal(ks[0], (B, L, D), dtype=jnp.float32)
        Wq = jax.random.normal(ks[1], (D, H, HD), dtype=jnp.float32) * s(D)
        Wkv_down = jax.random.normal(ks[2], (D, LD), dtype=jnp.float32) * s(D)
        Wk_up = jax.random.normal(ks[3], (LD, H, HD), dtype=jnp.float32) * s(LD)
        Wv_up = jax.random.normal(ks[4], (LD, H, HD), dtype=jnp.float32) * s(LD)
        Wout = jax.random.normal(ks[5], (H, HD, D), dtype=jnp.float32) * s(H * HD)
        return {'x_bld': x_bld, 'Wq': Wq, 'Wkv_down': Wkv_down, 'Wk_up': Wk_up, 'Wv_up': Wv_up, 'Wout': Wout}
    _L0_attn_all = _L0_attn_setup()
    _L0_attn_in = {k: v for k, v in _L0_attn_all.items() if k in ('Wq', 'Wkv_down', 'Wk_up', 'Wv_up', 'Wout')}
    del _L0_attn_all

    def _L0_cond2_setup():
        import jax, jax.numpy as jnp
        import numpy as np
        INPUT_DIM = 128
        HIDDEN_DIM = 128
        CHUNK_SIZE = 4

        def _linear_params(key, fan_in, fan_out):
            kw, kb = jax.random.split(key)
            bound = 1.0 / np.sqrt(fan_in)
            W = jax.random.uniform(kw, (fan_in, fan_out), jnp.float32, -bound, bound)
            b = jax.random.uniform(kb, (fan_out,), jnp.float32, -bound, bound)
            return (W, b)

        def _gru_forward(x, h0, Wz, bz, Wr, br, Wh, bh, Wp, bp):
            B, T, D = x.shape
            t = jnp.arange(T)
            do_prop = ((t + 1) % CHUNK_SIZE == 0) & (t < T - 1)
            xs = jnp.transpose(x, (1, 0, 2))

            def step(h, inp):
                x_t, prop = inp
                comb = jnp.concatenate([x_t, h], axis=-1)
                z = jax.nn.sigmoid(comb @ Wz + bz)
                r = jax.nn.sigmoid(comb @ Wr + br)
                comb2 = jnp.concatenate([x_t, r * h], axis=-1)
                h_cand = jnp.tanh(comb2 @ Wh + bh)
                h_new = (1.0 - z) * h + z * h_cand
                h_next = jnp.where(prop, jnp.tanh(h_new @ Wp + bp), h_new)
                return (h_next, h_new)
            _, ys = jax.lax.scan(step, h0, (xs, do_prop))
            return jnp.transpose(ys, (1, 0, 2))
        key = jax.random.key(seed)
        ks = jax.random.split(key, 6)
        x = jax.random.normal(ks[0], (64, 64, INPUT_DIM), jnp.float32)
        h0 = jax.random.normal(ks[1], (64, HIDDEN_DIM), jnp.float32)
        Wz, bz = _linear_params(ks[2], INPUT_DIM + HIDDEN_DIM, HIDDEN_DIM)
        Wr, br = _linear_params(ks[3], INPUT_DIM + HIDDEN_DIM, HIDDEN_DIM)
        Wh, bh = _linear_params(ks[4], INPUT_DIM + HIDDEN_DIM, HIDDEN_DIM)
        Wp, bp = _linear_params(ks[5], HIDDEN_DIM, HIDDEN_DIM)
        return {'x': x, 'h0': h0, 'Wz': Wz, 'bz': bz, 'Wr': Wr, 'br': br, 'Wh': Wh, 'bh': bh, 'Wp': Wp, 'bp': bp}
    _L0_cond2_all = _L0_cond2_setup()
    _L0_cond2_in = {k: v for k, v in _L0_cond2_all.items() if k in ('Wz', 'bz', 'Wr', 'br', 'Wh', 'bh', 'Wp', 'bp')}
    del _L0_cond2_all

    def _L0_ffn_setup():
        import jax, jax.numpy as jnp
        import numpy as np
        EMBED_DIM = 128
        HIDDEN_DIM = 512
        NUM_EXPERTS = 8
        TOP_K = 2
        key = jax.random.key(seed)
        k_x, k_g, k_w1, k_w2 = jax.random.split(key, 4)
        x = jax.random.normal(k_x, (2, 64, EMBED_DIM), dtype=jnp.float32)
        gate_w = jax.random.normal(k_g, (NUM_EXPERTS, EMBED_DIM), dtype=jnp.float32) * (1.0 / np.sqrt(EMBED_DIM))
        w1 = jax.random.normal(k_w1, (NUM_EXPERTS, EMBED_DIM, HIDDEN_DIM), dtype=jnp.float32) * np.sqrt(2.0 / EMBED_DIM)
        b1 = jnp.zeros((NUM_EXPERTS, HIDDEN_DIM), dtype=jnp.float32)
        w2 = jax.random.normal(k_w2, (NUM_EXPERTS, HIDDEN_DIM, EMBED_DIM), dtype=jnp.float32) * np.sqrt(2.0 / HIDDEN_DIM)
        b2 = jnp.zeros((NUM_EXPERTS, EMBED_DIM), dtype=jnp.float32)
        return {'x': x, 'gate_w': gate_w, 'w1': w1, 'b1': b1, 'w2': w2, 'b2': b2}
    _L0_ffn_all = _L0_ffn_setup()
    _L0_ffn_in = {k: v for k, v in _L0_ffn_all.items() if k in ('gate_w', 'w1', 'b1', 'w2', 'b2')}
    del _L0_ffn_all
    return {'x': x, 'cond_1024': cond_1024, 'L0_cond_Wx': _L0_cond_in['Wx'], 'L0_cond_Wh': _L0_cond_in['Wh'], 'L0_cond_b': _L0_cond_in['b'], 'L0_attn_Wq': _L0_attn_in['Wq'], 'L0_attn_Wkv_down': _L0_attn_in['Wkv_down'], 'L0_attn_Wk_up': _L0_attn_in['Wk_up'], 'L0_attn_Wv_up': _L0_attn_in['Wv_up'], 'L0_attn_Wout': _L0_attn_in['Wout'], 'L0_cond2_Wz': _L0_cond2_in['Wz'], 'L0_cond2_bz': _L0_cond2_in['bz'], 'L0_cond2_Wr': _L0_cond2_in['Wr'], 'L0_cond2_br': _L0_cond2_in['br'], 'L0_cond2_Wh': _L0_cond2_in['Wh'], 'L0_cond2_bh': _L0_cond2_in['bh'], 'L0_cond2_Wp': _L0_cond2_in['Wp'], 'L0_cond2_bp': _L0_cond2_in['bp'], 'L0_ffn_gate_w': _L0_ffn_in['gate_w'], 'L0_ffn_w1': _L0_ffn_in['w1'], 'L0_ffn_b1': _L0_ffn_in['b1'], 'L0_ffn_w2': _L0_ffn_in['w2'], 'L0_ffn_b2': _L0_ffn_in['b2']}

def reference(x, cond_1024, L0_cond_Wx, L0_cond_Wh, L0_cond_b, L0_attn_Wq, L0_attn_Wkv_down, L0_attn_Wk_up, L0_attn_Wv_up, L0_attn_Wout, L0_cond2_Wz, L0_cond2_bz, L0_cond2_Wr, L0_cond2_br, L0_cond2_Wh, L0_cond2_bh, L0_cond2_Wp, L0_cond2_bp, L0_ffn_gate_w, L0_ffn_w1, L0_ffn_b1, L0_ffn_w2, L0_ffn_b2):
    import jax
    import jax.numpy as jnp

    def _L0_cond_ref(x, h0, Wx, Wh, b):
        import jax, jax.numpy as jnp
        import numpy as np
        import math
        N, T, D, H = (64, 64, 128, 128)
        Hdim = h0.shape[1]
        c0 = jnp.zeros_like(h0)
        xW = jnp.einsum('ntd,dk->tnk', x, Wx) + b

        def step(carry, xw_t):
            prev_h, prev_c = carry
            a = xw_t + prev_h @ Wh
            i = jax.nn.sigmoid(a[:, :Hdim])
            f = jax.nn.sigmoid(a[:, Hdim:2 * Hdim])
            o = jax.nn.sigmoid(a[:, 2 * Hdim:3 * Hdim])
            g = jnp.tanh(a[:, 3 * Hdim:])
            next_c = f * prev_c + i * g
            next_h = o * jnp.tanh(next_c)
            return ((next_h, next_c), next_h)
        _, hs = jax.lax.scan(step, (h0, c0), xW)
        return jnp.transpose(hs, (1, 0, 2))

    def _L0_attn_ref(x_bld, Wq, Wkv_down, Wk_up, Wv_up, Wout):
        import jax, jax.numpy as jnp
        import numpy as np
        B, L, D = (2, 256, 128)
        H, HD = (16, 64)
        LD = 32
        q_blhd = jnp.einsum('bld,dhk->blhk', x_bld, Wq)
        latent_bll = jnp.einsum('bld,dc->blc', x_bld, Wkv_down)
        k_blhd = jnp.einsum('blc,chk->blhk', latent_bll, Wk_up)
        v_blhd = jnp.einsum('blc,chk->blhk', latent_bll, Wv_up)
        attn = jnp.einsum('bqhd,bkhd->bhqk', q_blhd, k_blhd) / jnp.sqrt(jnp.asarray(HD, dtype=x_bld.dtype))
        l = x_bld.shape[1]
        mask = (jnp.arange(l)[None, :] <= jnp.arange(l)[:, None])[None, None]
        neg_inf = jnp.finfo(attn.dtype).min
        attn = jax.nn.softmax(jnp.where(mask, attn, neg_inf), axis=-1)
        y_blhd = jnp.einsum('bhqk,bkhd->bqhd', attn, v_blhd)
        return jnp.einsum('bqhd,hdo->bqo', y_blhd, Wout)

    def _L0_cond2_ref(x, h0, Wz, bz, Wr, br, Wh, bh, Wp, bp):
        import jax, jax.numpy as jnp
        import numpy as np
        INPUT_DIM = 128
        HIDDEN_DIM = 128
        CHUNK_SIZE = 4

        def _linear_params(key, fan_in, fan_out):
            kw, kb = jax.random.split(key)
            bound = 1.0 / np.sqrt(fan_in)
            W = jax.random.uniform(kw, (fan_in, fan_out), jnp.float32, -bound, bound)
            b = jax.random.uniform(kb, (fan_out,), jnp.float32, -bound, bound)
            return (W, b)

        def _gru_forward(x, h0, Wz, bz, Wr, br, Wh, bh, Wp, bp):
            B, T, D = x.shape
            t = jnp.arange(T)
            do_prop = ((t + 1) % CHUNK_SIZE == 0) & (t < T - 1)
            xs = jnp.transpose(x, (1, 0, 2))

            def step(h, inp):
                x_t, prop = inp
                comb = jnp.concatenate([x_t, h], axis=-1)
                z = jax.nn.sigmoid(comb @ Wz + bz)
                r = jax.nn.sigmoid(comb @ Wr + br)
                comb2 = jnp.concatenate([x_t, r * h], axis=-1)
                h_cand = jnp.tanh(comb2 @ Wh + bh)
                h_new = (1.0 - z) * h + z * h_cand
                h_next = jnp.where(prop, jnp.tanh(h_new @ Wp + bp), h_new)
                return (h_next, h_new)
            _, ys = jax.lax.scan(step, h0, (xs, do_prop))
            return jnp.transpose(ys, (1, 0, 2))
        return _gru_forward(x, h0, Wz, bz, Wr, br, Wh, bh, Wp, bp)

    def _L0_ffn_ref(x, gate_w, w1, b1, w2, b2):
        import jax, jax.numpy as jnp
        import numpy as np
        EMBED_DIM = 128
        HIDDEN_DIM = 512
        NUM_EXPERTS = 8
        TOP_K = 2
        orig_shape = x.shape
        xt = x.reshape(-1, EMBED_DIM)
        logits = xt @ gate_w.T
        probs = jax.nn.softmax(logits, axis=-1)
        top_w, top_i = jax.lax.top_k(probs, TOP_K)
        top_w = top_w / (top_w.sum(axis=-1, keepdims=True) + 1e-09)
        h = jnp.einsum('td,ndh->tnh', xt, w1) + b1
        h = jax.nn.gelu(h, approximate=False)
        out_all = jnp.einsum('tnh,nhd->tnd', h, w2) + b2
        sel = jnp.take_along_axis(out_all, top_i[:, :, None], axis=1)
        out = (sel * top_w[:, :, None]).sum(axis=1)
        return out.reshape(orig_shape)
    x = x + _L0_attn_ref(_L0_cond_ref(x, cond_1024, L0_cond_Wx, L0_cond_Wh, L0_cond_b), L0_attn_Wq, L0_attn_Wkv_down, L0_attn_Wk_up, L0_attn_Wv_up, L0_attn_Wout)
    x = x + _L0_ffn_ref(_L0_cond2_ref(x, cond_1024, L0_cond2_Wz, L0_cond2_bz, L0_cond2_Wr, L0_cond2_br, L0_cond2_Wh, L0_cond2_bh, L0_cond2_Wp, L0_cond2_bp), L0_ffn_gate_w, L0_ffn_w1, L0_ffn_b1, L0_ffn_w2, L0_ffn_b2)
    return x

_drawn_inputs = setup_inputs


def setup_inputs(seed=0):
    import zlib

    import numpy as np

    out = dict(_drawn_inputs(seed))
    spreads = {'L0_cond_b': (0.0, 0.1), 'L0_ffn_b1': (0.0, 0.1), 'L0_ffn_b2': (0.0, 0.1)}
    factors = {'L0_attn_Wq': 7.77, 'L0_attn_Wk_up': 6.464, 'L0_cond2_bz': 3.005, 'L0_cond2_br': 20.435}
    for name, (base, spread) in spreads.items():
        noise = np.random.default_rng([zlib.crc32(name.encode()), seed]).standard_normal(out[name].shape)
        drawn = base * np.exp(spread * noise) if base else spread * noise
        out[name] = jnp.asarray(drawn.astype(out[name].dtype))
    for name, factor in factors.items():
        out[name] = (out[name] * factor).astype(out[name].dtype)
    return out
```

```python
import numpy as np
import concourse.bass as bass
from concourse import mybir
from contextlib import ExitStack

B, T, D = 16, 128, 128
H, HD, LD = 16, 64, 32
E, F = 8, 512
GS = 8
TOK = GS * B
NG = T // GS
TB = 32
NBLK = T // TB
HQ = 128 // TB
HG = H // HQ
BQ = B // (TB // GS)
PAD = T * B
FC = F // 128
NEG = -1.0e30
SH = 256.0
SW = 256.0
SP = SH * SW


def build(nc, a, out):
    f32 = mybir.dt.float32
    f16 = mybir.dt.float16
    bf16 = mybir.dt.bfloat16
    ALU = mybir.AluOpType
    ACT = mybir.ActivationFunctionType
    AX = mybir.AxisListType
    ds = bass.ds

    ctx = ExitStack()
    with ctx:
        def sb(name, shape, dt=f32):
            return ctx.enter_context(nc.sbuf_tensor(name, shape, dt))

        def pb(name, shape, dt=f32):
            return ctx.enter_context(nc.psum_tensor(name, shape, dt))

        def sem(name):
            return ctx.enter_context(nc.semaphore(name))

        ident = sb("ident", [128, 128])
        ident16 = sb("ident16", [128, 128], bf16)
        ind32 = sb("ind32", [12, 4 * TOK])
        ind = sb("ind", [12, 4 * TOK], bf16)
        gscale = sb("gscale", [4, 2])
        mask32 = sb("mask32", [128, TB])
        cmask = sb("cmask", [128, HG, TB], bf16)
        xT = sb("xT", [128, PAD + TB * B + B])
        h0T = sb("h0T", [128, B])
        lWx = sb("lWx", [128, 4, 128])
        lWh = sb("lWh", [128, 4, 128])
        bias = sb("bias", [4, 2, 128])
        bres = sb("bres", [4, 2, 128])
        bpart = [sb(f"bpart{n}", [4, 2, 128], bf16) for n in range(3)]
        biasP = sb("biasP", [12, 2, 128], bf16)
        b1 = sb("b1", [128, E, FC])
        b2 = sb("b2", [1, E * D])
        b2res = sb("b2res", [1, E * D])
        b2part = [sb(f"b2part{n}", [1, E * D], bf16) for n in range(3)]
        b2P = sb("b2P", [3, E * D], bf16)
        ones3 = sb("ones3", [3, 128], bf16)
        WqT = sb("WqT", [HD, H, D])
        WkT = sb("WkT", [HD, H, LD])
        WvT = sb("WvT", [HD, H, LD])
        Wout = sb("Wout", [HD, H, D])
        Wkvd = sb("Wkvd", [128, HQ, LD])
        Wqk = sb("Wqk", [128, H, LD])
        Wvo = sb("Wvo", [128, HG, D])
        gWx = sb("gWx", [128, 3, 128])
        gWh = sb("gWh", [128, 3, 128])
        gW1 = sb("gW1", [128, 3, 128])
        gW2 = sb("gW2", [128, 3, 128])
        gWhi = sb("gWhi", [128, 2, 128], f16)
        gWlo = sb("gWlo", [128, 2, 128], f16)
        lWhi = sb("lWhi", [128, 4, 128], f16)
        lWlo = sb("lWlo", [128, 4, 128], f16)
        w1hi = sb("w1hi", [128, E, F], f16)
        w1lo = sb("w1lo", [128, E, F], f16)
        gWp = sb("gWp", [128, 128])
        gateW = sb("gateW", [128, E])
        w1 = sb("w1", [128, E, F])
        w2 = sb("w2", [128, E, FC, D])

        h16 = sb("h16", [128, 2 * GS, B])
        hhi = sb("hhi", [128, B], f16)
        hlo = sb("hlo", [128, B], f16)
        oK = sb("oK", [128, B])
        c2 = sb("c2", [128, B])
        lT = sb("lT", [128, 4, B])
        lA = sb("lA", [128, B])
        lB = sb("lB", [128, B])
        lC = sb("lC", [128, B])
        latT = sb("latT", [128, B, GS + T])
        latS = sb("latS", [128, BQ, TB])
        latR = sb("latR", [128, BQ, LD])
        latN = sb("latN", [128, B, LD + 1])
        qT = sb("qT", [128, 2, HG, B, TB])
        qbd = sb("qbd", [128, 2, HG, HQ, TB])
        mx = sb("mx", [128, 2, HG])
        P = sb("P", [128, 2, HG, T])
        PTs = sb("PTs", [128, 2, HG, 128])
        rs = sb("rs", [128, HG])
        On = sb("On", [128, HG, LD])
        OT = sb("OT", [128, HG, BQ, TB])
        x1T = sb("x1T", [128, TOK + PAD + TB * B + B])
        g8 = sb("g8", [128, 2 * GS, B])
        ghi = sb("ghi", [128, 2 * GS, B], f16)
        glo = sb("glo", [128, 2 * GS, B], f16)
        zK = sb("zK", [128, B])
        gp = sb("gp", [128, B])
        gT = sb("gT", [128, 2, B])
        gRH = sb("gRH", [128, B])
        gA = sb("gA", [128, B])
        gC = sb("gC", [128, B])
        gB = sb("gB", [128, B])
        tri = sb("tri", [128, E, E])
        stx = sb("stx", [128, TOK])
        xn = sb("xn", [128, D])
        hidA = sb("hidA", [128, 2, TOK])
        hidB = sb("hidB", [128, 2, TOK])
        lg = sb("lg", [128, E])
        lmax = sb("lmax", [128, 1])
        low = sb("low", [128, E])
        th = sb("th", [128, E])
        eq = sb("eq", [128, E, E])
        gt = sb("gt", [128, E, E])
        rank = sb("rank", [128, E])
        den = sb("den", [128, E])
        ex = sb("ex", [128, E])
        picked = sb("picked", [128, E])
        sums = sb("sums", [128, 4])
        gates = sb("gates", [128, 2, E])
        acc = sb("acc", [128, 2, D])

        pL = [pb(f"pL{n}", [128, 4, GS, B]) for n in range(2)]
        p2 = pb("p2", [128, 512])
        p3 = pb("p3", [128, 512])
        p4 = pb("p4", [128, 512])
        p5 = pb("p5", [128, 512])
        p6 = pb("p6", [128, 512])
        p7 = pb("p7", [128, 512])
        pS = [p2, p3]
        pT, pQ, pO, pM = p4, p5, p6, p7
        pG = pL
        pHA, pHB, pY, pR = p2, p3, [p4, p5], p6

        loaded = sem("loaded")
        loaded2 = sem("loaded2")
        set_pool = sem("set_pool")
        set_dve = sem("set_dve")
        set_act = sem("set_act")
        fold_mm = sem("fold_mm")
        folded = sem("folded")
        split = sem("split")
        stacked = sem("stacked")
        opened = sem("opened")
        l_gates = sem("l_gates")
        l_tanh = sem("l_tanh")
        l_mul = sem("l_mul")
        l_c = sem("l_c")
        l_tc = sem("l_tc")
        l_h = sem("l_h")
        l_hi = sem("l_hi")
        l_lo = sem("l_lo")
        l_ok = sem("l_ok")
        g_hi = sem("g_hi")
        g_lo = sem("g_lo")
        g_zk = sem("g_zk")
        w1_split = sem("w1_split")
        lat_mm = sem("lat_mm")
        q_mm = sem("q_mm")
        lat_done = sem("lat_done")
        q_done = sem("q_done")
        lat_staged = sem("lat_staged")
        lat_turned = sem("lat_turned")
        latn_done = sem("latn_done")
        qbd_done = sem("qbd_done")
        s_mm = sem("s_mm")
        mx_done = sem("mx_done")
        sub_done = sem("sub_done")
        exp_done = sem("exp_done")
        pt_mm = sem("pt_mm")
        pt_done = sem("pt_done")
        o_mm = sem("o_mm")
        rs_done = sem("rs_done")
        on_done = sem("on_done")
        ot_done = sem("ot_done")
        proj_mm = sem("proj_mm")
        x1_done = sem("x1_done")
        g_rz = sem("g_rz")
        g_tanh = sem("g_tanh")
        g_rh = sem("g_rh")
        g_a = sem("g_a")
        g_cand = sem("g_cand")
        g_c = sem("g_c")
        g_b = sem("g_b")
        g_h = sem("g_h")
        g_prop = sem("g_prop")
        g_p = sem("g_p")
        stx_done = sem("stx_done")
        r_mm = sem("r_mm")
        route = sem("route")
        th_done = sem("th_done")
        l1a = sem("l1a")
        l1b = sem("l1b")
        gelu_a = sem("gelu_a")
        gelu_b = sem("gelu_b")
        l2a = sem("l2a")
        l2b = sem("l2b")
        acc_done = sem("acc_done")
        stored = [sem(f"stored{n}") for n in range(2)]

        block = ctx.enter_context(nc.Block())

        def whole(t):
            return t[tuple(slice(None) for _ in t.shape)]

        LOADS = [(ident, "ident"), (ind32, "ind"), (gscale, "gscale"), (bias, "bias"), (h0T, "h0T"),
                 (lWx, "lWx"), (lWh, "lWh")]
        LOADS2 = [(WqT, "WqT"), (WkT, "WkT"), (WvT, "WvT"), (Wout, "Wout"), (mask32, "mask"), (b2, "b2"),
                  (gWx, "gWx"), (gWh, "gWh"), (gWp, "gWp"), (gateW, "gateW"), (tri, "tri"), (b1, "b1")]
        N1 = 16 * (len(LOADS) + 1)
        N2 = 16 * (len(LOADS2) + HQ + 2)
        CLEARED = [P, h16, c2, latT, latS, qT, qbd, latN, OT, stx, hidA, hidB, g8, ghi, glo, acc, gates]
        NSET = len(CLEARED) + 4
        SETD = 2 + 4 + 4 + 2 + 2
        SETA = 19
        ROUTE = 18

        @block.sync
        def _(sp):
            sp.sem_inc(stored[0], 16)
            sp.dma_start(xT[:, 0:PAD], a["xT"]).then_inc(loaded, 16)
            for t, name in LOADS:
                sp.dma_start(whole(t), a[name]).then_inc(loaded, 16)
            for t, name in LOADS2:
                sp.dma_start(whole(t), a[name]).then_inc(loaded2, 16)
            for q in range(HQ):
                sp.dma_start(Wkvd[:, q, :], a["Wkvd"]).then_inc(loaded2, 16)
            sp.dma_start(whole(w1), a["w1"]).then_inc(loaded2, 16)
            sp.dma_start(whole(w2), a["w2"]).then_inc(loaded2, 16)
            sp.wait_ge(split, 1)
            for n in range(3):
                sp.dma_start(biasP[4 * n:4 * n + 4, :, :], whole(bpart[n])).then_inc(stacked, 16)
            sp.wait_ge(split, 2)
            for n in range(3):
                sp.dma_start(b2P[n:n + 1, :], whole(b2part[n])).then_inc(stacked, 16)
            with sp.Fori(0, NG // 2) as i:
                for hf in range(2):
                    sp.wait_ge(acc_done, 16 * i + (8 * hf + 4) + 1)
                    sp.dma_start(out[ds(i * (2 * TOK) + hf * TOK, TOK), :], acc[:, 1 - hf, :]).then_inc(stored[1 - hf], 16)
            for hf in range(2):
                sp.wait_ge(acc_done, 8 * (NG + hf) + 4 + 1)
                sp.dma_start(out[(NG + hf) * TOK:(NG + hf + 1) * TOK, :], acc[:, 1 - hf, :]).then_inc(stored[1 - hf], 16)
            for n in range(2):
                sp.wait_ge(stored[n], 16 * (NG // 2 + 2 - n))

        @block.gpsimd
        def _(pool):
            pool.sem_inc(latn_done, 1)
            for t in CLEARED:
                pool.memset(whole(t), 0.0).then_inc(set_pool, 1)
            pool.memset(xT[:, PAD:], 0.0).then_inc(set_pool, 1)
            pool.memset(whole(x1T), 0.0).then_inc(set_pool, 1)
            pool.memset(whole(ones3), 1.0).then_inc(set_pool, 1)
            pool.wait_ge(set_pool, NSET - 1)
            pool.memset(latN[:, :, LD:LD + 1], 1.0).then_inc(set_pool, 1)
            pool.wait_ge(loaded2, N2)
            pool.tensor_scalar(whole(w1hi), whole(w1), SW, None, ALU.mult).then_inc(w1_split, 1)
            pool.tensor_scalar(whole(w1), whole(w1), SW, None, ALU.mult).then_inc(w1_split, 1)
            pool.wait_ge(w1_split, 2)
            pool.tensor_tensor(whole(w1lo), whole(w1), whole(w1hi), ALU.subtract).then_inc(w1_split, 1)
            pool.wait_ge(w1_split, 3)
            for j in range(NBLK):
                rows = slice(TB * j, TB * (j + 1))
                with pool.Fori(0, 2) as i:
                    for hf in range(2):
                        turn = 2 * i + (4 * j + hf)
                        b0 = 2 * BQ * i + BQ * hf
                        pool.wait_ge(lat_done, 4 * (j + 1) + 1 + 1)
                        pool.wait_ge(lat_turned, turn + 1)
                        pool.tensor_copy(latS[rows, :, :],
                                         latT[rows, ds(b0, BQ), GS + TB * j:GS + TB * (j + 1)]).then_inc(lat_staged, 1)
                        pool.wait_ge(q_done, 4 * (j + 1) + 1 + 1)
                        for k in range(BQ):
                            if k == 2:
                                pool.wait_ge(lat_turned, turn + 1 + 1)
                                pool.tensor_copy(latN[rows, ds(b0, BQ), 0:LD], latR[rows, :, :]).then_inc(latn_done, 1)
                            pool.wait_ge(s_mm, BQ * turn + (k + 1))
                            for q in range(HQ):
                                r = slice(32 * q, 32 * q + 32)
                                pool.tensor_copy(qbd[r, k % 2, :, q, :], qT[r, j % 2, :, ds(b0 + k, 1), :]
                                                 .rearrange("p g o t -> p g (o t)")).then_inc(qbd_done, 1)

            def stage(G, off):
                pool.wait_ge(r_mm, 2 * G + 1)
                pool.tensor_copy(whole(stx), x1T[:, off]).then_inc(stx_done, 1)

            pool.wait_ge(x1_done, 4 * NBLK + 1)
            with pool.Fori(0, NG // 2) as i:
                for hf in range(2):
                    stage(2 * i + hf, ds(i * (2 * TOK) + hf * TOK, TOK))
            stage(NG, slice(NG * TOK, (NG + 1) * TOK))

        @block.tensor
        def _(pe):
            def mm(out, lhsT, rhs, start=False, stop=True):
                return nc.tensor.matmul(out, lhsT=lhsT, rhs=rhs, start=start, stop=stop, skip_group_check=True)

            def flat(t):
                return t.rearrange("p a b -> p (a b)")

            pe.sem_inc(s_mm, 2)
            pe.sem_inc(pt_mm, 2)
            for x in (r_mm, l1a, l1b, l2a, l2b):
                pe.sem_inc(x, 1)
            pe.wait_ge(loaded2, N2)
            for h in range(H):
                mm(p2[:, LD * h:LD * (h + 1)], WqT[:, h, :], WkT[:, h, :], start=True)
            for h in range(H):
                q, g = h % HQ, h // HQ
                last = mm(p3[32 * q:32 * q + 32, D * g:D * (g + 1)], WvT[:, h, :], Wout[:, h, :], start=True)
            last.then_inc(fold_mm, 1)
            pe.wait_ge(set_pool, NSET)
            pe.wait_ge(set_dve, SETD)
            pe.wait_ge(set_act, SETA)
            pe.wait_ge(stacked, 16 * 6)

            def l_fill(G, hf, g):
                if g == 0:
                    mm(pL[hf][:, :, :, :].rearrange("p g s b -> p (g s b)"), biasP[:, 0, :], ind[:, :], start=True)
                return mm(pL[hf][:, g, :, :].rearrange("p s b -> p (s b)"), lWx[:, g, :], xT[:, ds(G * TOK, TOK)])

            for g in range(4):
                l_fill(0, 0, g)

            def lat_q(turn, hf):
                src = h16[:, GS * (1 - hf):GS * (2 - hf), :].rearrange("p s b -> p (s b)")
                pe.wait_ge(l_h, GS * turn + 1)
                pe.wait_ge(lat_done, turn + 1)
                pe.wait_ge(q_done, turn + 1)
                mm(pM[:, 0:TOK], flat(Wkvd[:, :, :]), src, start=True).then_inc(lat_mm, 1)
                for g in range(HG):
                    last = mm(pQ[:, TOK * g:TOK * (g + 1)], flat(Wqk[:, HQ * g:HQ * (g + 1), :]), src, start=True)
                last.then_inc(q_mm, 1)

            def project(turn):
                pe.wait_ge(ot_done, BQ * turn + 1)
                for g in range(HG):
                    last = mm(pO[:, 256:256 + TOK], Wvo[:, g, :], flat(OT[:, g, :, :]), start=(g == 0))
                last.then_inc(proj_mm, 1)

            def scores(n, k, L, b):
                pe.wait_ge(qbd_done, 4 * n + 4)
                pe.wait_ge(sub_done, n + 1)
                S = pS[k % 2]
                mm(S[:, :].rearrange("p (g t) -> p g t", g=HG)[:, :, L - TB:L], ident16[:, :],
                   cmask[:, :, :], start=True)
                for g in range(HG):
                    last = mm(S[:, T * g:T * g + L], flat(qbd[:, k % 2, g, :, :]),
                              latT[:, ds(b, 1), GS:GS + L].rearrange("p o t -> p (o t)"))
                last.then_inc(s_mm, 1)

            def turn_probs(n, k, L):
                pe.wait_ge(exp_done, n + 1)
                pe.wait_ge(pt_done, n + 1)
                for g in range(HG):
                    last = nc.tensor.transpose(pT[:, 128 * g:128 * (g + 1)], P[:, k % 2, g, :], ident[:, :])
                last.then_inc(pt_mm, 1)

            def values(n, k, L, b, turn):
                pe.wait_ge(pt_done, n + 1 + 1)
                if k == 0:
                    pe.wait_ge(latn_done, turn + 1 + 1)
                    pe.wait_ge(x1_done, turn + 1)
                pe.wait_ge(on_done, n + 1)
                for g in range(HG):
                    last = mm(pO[:, (LD + 1) * g:(LD + 1) * (g + 1)], PTs[0:L, k % 2, g, :],
                              latN[0:L, ds(b, 1), :].rearrange("p o c -> p (o c)"), start=(g == 0))
                last.then_inc(o_mm, 1)

            def attention(s, turn, L, b0):
                if s == 0:
                    project(turn)
                if 1 <= s <= 4:
                    scores(BQ * turn + (s - 1), s - 1, L, b0 + (s - 1))
                if 4 <= s <= 7:
                    values(BQ * turn + (s - 4), s - 4, L, b0 + (s - 4), turn)
                if 3 <= s <= 6:
                    turn_probs(BQ * turn + (s - 3), s - 3, L)

            for p in range(NBLK + 1):
                if p == NBLK:
                    lat_q(4 * NBLK, 0)
                with pe.Fori(0, 2) as i:
                    for hf in range(2):
                        G = 2 * i + (4 * p + hf)
                        for s in range(GS):
                            if p < NBLK:
                                pe.wait_ge(l_hi, GS * G + (s + 1))
                                for g in range(4):
                                    mm(pL[hf][:, g, s, :], lWhi[:, g, :], hhi[:, :])
                                    mm(pL[hf][:, g, s, :], lWlo[:, g, :], hhi[:, :])
                                pe.wait_ge(l_lo, GS * G + (s + 1))
                                for g in range(4):
                                    last = mm(pL[hf][:, g, s, :], lWhi[:, g, :], hlo[:, :])
                                last.then_inc(l_gates, 1)
                                if s == 0:
                                    lat_q(G, hf)
                                if s in (1, 2, 5, 6):
                                    l_fill(G + 1, 1 - hf, (1, 2, 5, 6).index(s))
                            if p > 0:
                                attention(s, G - 4, TB * p, 2 * BQ * i + BQ * hf)
            project(4 * NBLK)

            def g_fill(G, hf, g):
                if g == 0:
                    mm(pG[hf][:, :, :, :].rearrange("p g s b -> p (g s b)"), biasP[:, 1, :], ind[:, :], start=True)
                return mm(pG[hf][:, g, :, :].rearrange("p s b -> p (s b)"), gWx[:, g, :], x1T[:, ds(G * TOK + TOK, TOK)])

            pe.wait_ge(x1_done, 4 * NBLK + 1)
            for g in range(3):
                g_fill(0, 0, g)
            mm(pY[1][:, :], ones3[:, :], b2P[:, 512:1024], start=True)
            mm(pHB[:, 0:2 * TOK], biasP[:, 1, :], ind[:, 0:2 * TOK], start=True).then_inc(opened, 1)
            pe.wait_ge(w1_split, 3)

            def route_x(G, hf):
                pe.wait_ge(acc_done, 8 * G + 1)
                pe.wait_ge(stx_done, G + 1)
                mm(pR[:, 0:E], g8[:, GS * (1 - hf):GS * (2 - hf), :].rearrange("p s b -> p (s b)"), gateW[:, :],
                   start=True).then_inc(r_mm, 1)
                nc.tensor.transpose(pR[:, 128:256], stx[:, :], ident[:, :]).then_inc(r_mm, 1)

            def layer1(G, hf, e, half):
                bank, free, done = ((pHA, gelu_a, l1a), (pHB, gelu_b, l1b))[half]
                pe.wait_ge(free, E * G + (e + half) + 1)
                hi, lo = (t[:, GS * (1 - hf):GS * (2 - hf), :].rearrange("p s b -> p (s b)") for t in (ghi, glo))
                for c in range(2):
                    Y, cols = bank[:, TOK * c:TOK * (c + 1)], slice(128 * (2 * half + c), 128 * (2 * half + c + 1))
                    mm(Y, w1hi[:, e, cols], hi, start=(c == 0))
                    mm(Y, w1hi[:, e, cols], lo)
                    last = mm(Y, w1lo[:, e, cols], hi)
                last.then_inc(done, 1)

            def layer2(G, e, half):
                hid, ready, done = ((hidA, gelu_a, l2a), (hidB, gelu_b, l2b))[half]
                Y = pY[e // 4]
                if half == 0 and e % 4 == 0:
                    pe.wait_ge(acc_done, 8 * G + e + 1)
                    mm(Y[:, :], ones3[:, :], b2P[:, 512 * (e // 4):512 * (e // 4) + 512], start=True)
                pe.wait_ge(ready, E * G + ((e + 1) % E + half) + 1)
                for c in range(2):
                    last = mm(Y[:, D * (e % 4):D * (e % 4 + 1)], hid[:, c, :], w2[:, e, 2 * half + c, :])
                last.then_inc(done, 1)

            def gru_turn(i, hf, gru, experts, steps=GS):
                G = 2 * i + hf
                for s in range(steps):
                    if gru:
                        if s % 4 == 0:
                            pe.wait_ge(g_p, 2 * G + (s // 4 + 1))
                            W = gW1
                            for g in range(2):
                                last = mm(pG[hf][:, g, s, :], W[:, g, :], gp[:, :])
                        else:
                            W = gW2
                            pe.wait_ge(g_hi, GS * G + s)
                            for g in range(2):
                                mm(pG[hf][:, g, s, :], gWhi[:, g, :], ghi[:, GS * hf + s - 1, :])
                                mm(pG[hf][:, g, s, :], gWlo[:, g, :], ghi[:, GS * hf + s - 1, :])
                            pe.wait_ge(g_lo, GS * G + (s + 1))
                            for g in range(2):
                                last = mm(pG[hf][:, g, s, :], gWhi[:, g, :], glo[:, GS * hf + s - 1, :])
                        last.then_inc(g_rz, 1)
                    if experts and s == 0:
                        pe.wait_ge(g_lo, GS * G + 1)
                    if s == 0 and experts:
                        route_x(G, hf)
                    if experts:
                        layer1(G, hf, s, 0)
                    layer2(G, (s - 1) % E, 0)
                    if gru:
                        pe.wait_ge(g_rh, GS * G + (s + 1))
                        mm(pG[hf][:, 2, s, :], W[:, 2, :], gRH[:, :]).then_inc(g_cand, 1)
                    if experts:
                        layer1(G, hf, s, 1)
                    layer2(G, (s - 1) % E, 1)
                    if gru:
                        if s in (0, 1, 2):
                            g_fill(G + 1, 1 - hf, s)
                        if s % 4 == 3:
                            pe.wait_ge(g_h, GS * G + (s + 1))
                            mm(pG[hf][:, 3, s, :], gWp[:, :], g8[:, GS * hf + s, :]).then_inc(g_prop, 1)

            with pe.Fori(0, NG // 2) as i:
                for hf in range(2):
                    gru_turn(i, hf, True, True)
            gru_turn(NG // 2, 0, False, True)
            gru_turn(NG // 2, 1, False, False, 1)

        @block.scalar
        def _(act):
            A = nc.scalar.activation
            for x in (q_done, pt_done, gelu_a, gelu_b):
                act.sem_inc(x, 1)
            act.wait_ge(loaded, N1)
            act.wait_ge(set_pool, NSET)
            A(h16[:, 2 * GS - 1, :], h0T[:, :], ACT.Copy, scale=SH).then_inc(set_act, 1)
            A(hhi[:, :], h0T[:, :], ACT.Copy, scale=SH).then_inc(set_act, 1)
            A(ident16[:, :], ident[:, :], ACT.Copy).then_inc(set_act, 1)
            A(ind[:, :], ind32[:, :], ACT.Copy).then_inc(set_act, 1)
            A(lWh[:, 0:3, :], lWh[:, 0:3, :], ACT.Copy, scale=0.5 * SW).then_inc(set_act, 1)
            A(lWh[:, 3, :], lWh[:, 3, :], ACT.Copy, scale=SW).then_inc(set_act, 1)
            act.wait_ge(set_act, 6)
            A(lWhi[:, :, :], lWh[:, :, :], ACT.Copy).then_inc(set_act, 1)
            A(lWx[:, 0:3, :], lWx[:, 0:3, :], ACT.Copy, scale=0.5 * SP).then_inc(set_act, 1)
            A(lWx[:, 3, :], lWx[:, 3, :], ACT.Copy, scale=SP).then_inc(set_act, 1)
            act.wait_ge(loaded2, N2)
            A(Wkvd[:, :, :], Wkvd[:, :, :], ACT.Copy, scale=1.0 / SH).then_inc(set_act, 1)
            A(gW1[:, :, :], gWh[:, :, :], ACT.Copy, scale=0.5 * SP).then_inc(set_act, 1)
            A(gW2[:, :, :], gWh[:, :, :], ACT.Copy, scale=0.5 * SW).then_inc(set_act, 1)
            A(gWhi[:, :, :], gWh[:, 0:2, :], ACT.Copy, scale=0.5 * SW).then_inc(set_act, 1)
            A(gWx[:, 0:2, :], gWx[:, 0:2, :], ACT.Copy, scale=0.5 * SP).then_inc(set_act, 1)
            A(gWx[:, 2, :], gWx[:, 2, :], ACT.Copy, scale=SP).then_inc(set_act, 1)
            A(gWp[:, :], gWp[:, :], ACT.Copy, scale=SW).then_inc(set_act, 1)
            A(gateW[:, :], gateW[:, :], ACT.Copy, scale=1.0 / SH).then_inc(set_act, 1)
            A(gp[:, :], h0T[:, :], ACT.Copy).then_inc(g_p, 1)
            act.wait_ge(fold_mm, 1)
            A(Wqk[:, :, :].rearrange("p h c -> p (h c)"), p2[:, :], ACT.Copy, scale=1.0 / SH / HD ** 0.5).then_inc(set_act, 1)
            A(Wvo[:, :, :].rearrange("p g d -> p (g d)"), p3[:, :], ACT.Copy).then_inc(set_act, 1)

            def q_copy(turn, par, t0):
                act.wait_ge(q_mm, turn + 1)
                A(qT[:, ds(par, 1), :, :, ds(t0, GS)].rearrange("p o g b t -> p (o g) b t"), pQ[:, :].rearrange("p (g s b) -> p g b s", g=HG, b=B),
                  ACT.Copy).then_inc(q_done, 1)

            def exps(n, k, L):
                act.wait_ge(sub_done, n + 3)
                A(P[:, k % 2, :, 0:L], P[:, k % 2, :, 0:L], ACT.Exp).then_inc(exp_done, 1)

            def pt_copy(n, k, L):
                act.wait_ge(pt_mm, n + 3)
                A(PTs[0:L, k % 2, :, :].rearrange("p g q -> p (g q)"), pT[0:L, :], ACT.Copy).then_inc(pt_done, 1)

            for p in range(NBLK + 1):
                if p == NBLK:
                    q_copy(4 * NBLK, (NBLK - 1) % 2, TB - GS)
                with act.Fori(0, 2) as i:
                    for hf in range(2):
                        G = 2 * i + (4 * p + hf)
                        turn = 2 * i + (4 * p + hf - 4)
                        for s in range(GS):
                            if p < NBLK:
                                act.wait_ge(l_gates, GS * G + (s + 1))
                                A(lT[:, :, :], pL[hf][:, :, s, :], ACT.Tanh, scale=1.0 / SP).then_inc(l_tanh, 1)
                                act.wait_ge(l_c, GS * G + (s + 1))
                                A(lC[:, :], c2[:, :], ACT.Tanh, scale=0.5).then_inc(l_tc, 1)
                                if s == 0 and hf == 0:
                                    was, now = (p - 1) % 2, p % 2
                                    q_copy(G, i * (now - was) + was, i * (GS - (TB - GS)) + (TB - GS))
                                if s == 0 and hf == 1:
                                    q_copy(G, p % 2, 2 * GS * i)
                            if p > 0:
                                L = TB * p
                                if 2 <= s <= 5:
                                    exps(BQ * turn + (s - 2), s - 2, L)
                                if 3 <= s <= 6:
                                    pt_copy(BQ * turn + (s - 3), s - 3, L)

            def gelu(n, e, half, step):
                bank, hid, full, read, done = ((pHA, hidA, l1a, l2a, gelu_a), (pHB, hidB, l1b, l2b, gelu_b))[half]
                act.wait_ge(full, n + 1)
                act.wait_ge(read, step + 1)
                for c in range(2):
                    last = A(hid[:, c, :], bank[:, TOK * c:TOK * (c + 1)], ACT.Gelu,
                             bias=b1[:, e, 2 * half + c:2 * half + c + 1], scale=1.0 / SP)
                last.then_inc(done, 1)

            def gru_turn(i, hf, gru, experts, steps=GS):
                G = 2 * i + hf
                for s in range(steps):
                    if gru:
                        act.wait_ge(g_rz, GS * G + (s + 1))
                        A(gT[:, :, :], pG[hf][:, 0:2, s, :], ACT.Tanh, scale=1.0 / SP).then_inc(g_tanh, 1)
                    gelu(E * G + s, (s - 1) % E, 1, E * G + s)
                    if s == 3 and experts:
                        act.wait_ge(route, ROUTE * G + 4 + 1)
                        A(th[:, :], low[:, :], ACT.Tanh, scale=0.5).then_inc(th_done, 1)
                    if gru:
                        act.wait_ge(g_cand, GS * G + (s + 1))
                        A(gC[:, :], pG[hf][:, 2, s, :], ACT.Tanh, scale=1.0 / SP).then_inc(g_c, 1)
                    if experts:
                        gelu(E * G + (s + 1), s, 0, E * G + (s + 1))
                    if gru and s % 4 == 3:
                        act.wait_ge(g_prop, 2 * G + (s // 4 + 1))
                        A(gp[:, :], pG[hf][:, 3, s, :], ACT.Tanh, scale=1.0 / SP).then_inc(g_p, 1)

            act.wait_ge(opened, 1)
            with act.Fori(0, NG // 2) as i:
                for hf in range(2):
                    gru_turn(i, hf, True, True)
            gru_turn(NG // 2, 0, False, True)
            gru_turn(NG // 2, 1, False, False, 1)

        @block.vector
        def _(dve):
            V = nc.vector
            dve.sem_inc(sub_done, 2)
            for x in (lat_turned, lat_done, ot_done, on_done, acc_done, route):
                dve.sem_inc(x, 1)
            steps = [0]

            def link(ins):
                steps[0] += 1
                ins.then_inc(set_dve, 1)
                dve.wait_ge(set_dve, steps[0])

            def split3(x, res, parts):
                link(V.tensor_copy(whole(parts[0]), whole(x)))
                link(V.tensor_tensor(whole(res), whole(x), whole(parts[0]), ALU.subtract))
                link(V.tensor_copy(whole(parts[1]), whole(res)))
                link(V.tensor_tensor(whole(res), whole(res), whole(parts[1]), ALU.subtract))
                V.tensor_copy(whole(parts[2]), whole(res)).then_inc(split, 1)

            dve.wait_ge(loaded, N1)
            for n in range(2):
                link(V.tensor_scalar(bias[:, n, :], bias[:, n, :], gscale[:, n:n + 1], None, ALU.mult))
            split3(bias, bres, bpart)
            dve.wait_ge(set_act, 7)
            link(V.tensor_tensor(lWlo[:, :, :], lWh[:, :, :], lWhi[:, :, :], ALU.subtract))
            link(V.tensor_tensor(hlo[:, :], h16[:, 2 * GS - 1, :], hhi[:, :], ALU.subtract))
            dve.wait_ge(loaded2, N2)
            split3(b2, b2res, b2part)
            link(V.tensor_copy(cmask[:, :, :], mask32[:, :].unsqueeze(1).to_broadcast([128, HG, TB])))
            dve.wait_ge(set_act, SETA)
            link(V.tensor_tensor(gWlo[:, :, :], gW2[:, 0:2, :], gWhi[:, :, :], ALU.subtract))
            for x in (l_hi, l_lo, l_h, g_lo):
                dve.sem_inc(x, 1)
            assert steps[0] == SETD
            dve.wait_ge(set_pool, NSET)

            def lat_copy(n):
                dve.wait_ge(lat_mm, n + 1)
                V.tensor_copy(latT[:, :, ds(n * GS, GS)],
                              pM[:, 0:TOK].rearrange("p (s b) -> p b s", b=B)).then_inc(lat_done, 1)

            def add_x(turn, off):
                dve.wait_ge(proj_mm, turn + 1)
                V.tensor_tensor(x1T[:, ds(off + TOK, TB * B)].rearrange("p (t b) -> p b t", b=B)[:, 0:BQ, :],
                                pO[:, 256:256 + TOK].rearrange("p (b t) -> p b t", b=BQ),
                                xT[:, ds(off, TB * B)].rearrange("p (t b) -> p b t", b=B)[:, 0:BQ, :],
                                ALU.add).then_inc(x1_done, 1)

            def softmax_front(n, k, L):
                S = pS[k % 2][:, :].rearrange("p (g t) -> p g t", g=HG)[:, :, 0:L]
                dve.wait_ge(s_mm, n + 3)
                V.tensor_reduce(mx[:, k % 2, :], S, AX.X, ALU.max).then_inc(mx_done, 1)
                dve.wait_ge(mx_done, n + 1)
                dve.wait_ge(pt_mm, n + 1)
                V.tensor_tensor(P[:, k % 2, :, 0:L], S,
                                mx[:, k % 2, :].unsqueeze(2).to_broadcast([128, HG, L]), ALU.subtract).then_inc(sub_done, 1)

            def normalise(n, k, turn):
                O = pO[:, 0:HG * (LD + 1)].rearrange("p (g c) -> p g c", g=HG)
                dve.wait_ge(o_mm, n + 1)
                V.reciprocal(rs[:, :].unsqueeze(2), O[:, :, LD:LD + 1]).then_inc(rs_done, 1)
                dve.wait_ge(rs_done, n + 1)
                V.tensor_tensor(On[:, :, :], O[:, :, 0:LD], rs[:, :].unsqueeze(2).to_broadcast([128, HG, LD]),
                                ALU.mult).then_inc(on_done, 1)
                dve.wait_ge(on_done, n + 1 + 1)
                if k == 0:
                    dve.wait_ge(proj_mm, turn + 1)
                V.transpose(OT[:, :, k, :], On[:, :, :]).then_inc(ot_done, 1)

            for p in range(NBLK + 1):
                rows = slice(TB * (p - 1), TB * p)
                if p == NBLK:
                    lat_copy(4 * NBLK)
                with dve.Fori(0, 2) as i:
                    for hf in range(2):
                        G = 2 * i + (4 * p + hf)
                        turn = 2 * i + (4 * p + hf - 4)
                        for s in range(GS):
                            if p < NBLK:
                                slot = GS * hf + s
                                dve.wait_ge(l_tanh, GS * G + (s + 1))
                                V.scalar_tensor_tensor(lA[:, :], lT[:, 1, :], 1.0, c2[:, :], ALU.add, ALU.mult).then_inc(l_mul, 1)
                                V.scalar_tensor_tensor(lB[:, :], lT[:, 0, :], 1.0, lT[:, 3, :], ALU.add, ALU.mult).then_inc(l_mul, 1)
                                dve.wait_ge(l_mul, 2 * GS * G + (2 * s + 2))
                                V.scalar_tensor_tensor(c2[:, :], lA[:, :], 0.5, lB[:, :], ALU.mult, ALU.add).then_inc(l_c, 1)
                                V.tensor_scalar(oK[:, :], lT[:, 2, :], SH / 2, SH / 2, ALU.mult, ALU.add).then_inc(l_ok, 1)
                                dve.wait_ge(l_ok, GS * G + (s + 1))
                                dve.wait_ge(l_tc, GS * G + (s + 1))
                                V.tensor_tensor(hhi[:, :], oK[:, :], lC[:, :], ALU.mult).then_inc(l_hi, 1)
                                V.tensor_tensor(h16[:, slot, :], oK[:, :], lC[:, :], ALU.mult).then_inc(l_h, 1)
                                dve.wait_ge(l_hi, GS * G + (s + 2))
                                dve.wait_ge(l_h, GS * G + (s + 2))
                                V.tensor_tensor(hlo[:, :], h16[:, slot, :], hhi[:, :], ALU.subtract).then_inc(l_lo, 1)
                                if s == 0:
                                    lat_copy(G)
                            if p > 0:
                                L = TB * p
                                if s == 0:
                                    if hf == 0:
                                        was = TB * B * (p - 2 if p > 1 else NBLK) + 3 * BQ
                                        now = TB * B * (p - 1) + BQ
                                        add_x(turn, i * (now - was) + was)
                                    else:
                                        add_x(turn, i * (2 * BQ) + TB * B * (p - 1))
                                    dve.wait_ge(lat_staged, turn + 1)
                                    dve.wait_ge(latn_done, turn + 1)
                                    V.transpose(latR[rows, :, :], latS[rows, :, :]).then_inc(lat_turned, 1)
                                if 1 <= s <= 4:
                                    softmax_front(BQ * turn + (s - 1), s - 1, L)
                                if s >= 4:
                                    normalise(BQ * turn + (s - 4), s - 4, turn)
            add_x(4 * NBLK, TB * B * (NBLK - 1) + 3 * BQ)

            def routing(G, hf, s):
                li, lj = lg[:, :].unsqueeze(2).to_broadcast([128, E, E]), lg[:, :].unsqueeze(1).to_broadcast([128, E, E])
                ops = [
                    (0, lambda: V.tensor_copy(lg[:, :], pR[:, 0:E])),
                    (0, lambda: V.tensor_copy(xn[:, :], pR[:, 128:256])),
                    (1, lambda: V.tensor_reduce(lmax[:, :], lg[:, :], AX.X, ALU.max)),
                    (2, lambda: V.tensor_scalar(low[:, :], lg[:, :], lmax[:, 0:1], None, ALU.subtract)),
                    (2, lambda: V.tensor_tensor(eq[:, :, :], lj, li, ALU.is_equal)),
                    (2, lambda: V.tensor_tensor(gt[:, :, :], lj, li, ALU.is_gt)),
                    (3, lambda: V.tensor_tensor(eq[:, :, :], eq[:, :, :], tri[:, :, :], ALU.mult)),
                    (3, lambda: V.tensor_tensor(gt[:, :, :], gt[:, :, :], eq[:, :, :], ALU.add)),
                    (3, lambda: V.tensor_reduce(rank[:, :], gt[:, :, :], AX.X, ALU.add)),
                    (4, lambda: V.tensor_scalar(den[:, :], th[:, :], -1.0, 1.0, ALU.mult, ALU.add)),
                    (4, lambda: V.reciprocal(den[:, :], den[:, :])),
                    (4, lambda: V.scalar_tensor_tensor(ex[:, :], th[:, :], 1.0, den[:, :], ALU.add, ALU.mult)),
                    (4, lambda: V.tensor_reduce(sums[:, 0:1], ex[:, :], AX.X, ALU.add)),
                    (5, lambda: V.scalar_tensor_tensor(picked[:, :], rank[:, :], 2.0, ex[:, :], ALU.is_lt, ALU.mult)),
                    (5, lambda: V.tensor_reduce(sums[:, 1:2], picked[:, :], AX.X, ALU.add)),
                    (5, lambda: V.scalar_tensor_tensor(sums[:, 2:3], sums[:, 0:1], 1.0e-9, sums[:, 1:2], ALU.mult, ALU.add)),
                    (5, lambda: V.reciprocal(sums[:, 3:4], sums[:, 2:3])),
                    (5, lambda: V.tensor_scalar(gates[:, hf, :], picked[:, :], sums[:, 3:4], None, ALU.mult)),
                ]
                assert len(ops) == ROUTE
                for at, (step, op) in enumerate(ops):
                    if step != s:
                        continue
                    if at == 0:
                        dve.wait_ge(r_mm, 2 * G + 2 + 1)
                    if at == 9:
                        dve.wait_ge(th_done, G + 1)
                    dve.wait_ge(route, ROUTE * G + at + 1)
                    op().then_inc(route, 1)

            def combine(i, hf, slot, s):
                G = 2 * i + hf
                first = {5: 0, 6: 2, 1: 4, 2: 6}[s]
                Y = pY[first // 4][:, :].rearrange("p (e d) -> p e d", e=4)
                if s in (1, 5):
                    dve.wait_ge(l2b, E * G + s // 5 * 4 + 2)
                    dve.wait_ge(route, ROUTE * G + (ROUTE if s == 5 else 0) + 1)
                if s == 5:
                    dve.wait_ge(stored[hf], 16 * i + 16)
                for e in (first, first + 1):
                    old = xn[:, :] if e == 0 else acc[:, slot, :]
                    dve.wait_ge(acc_done, 8 * G + {5: 4, 6: 6, 1: 0, 2: 2}[s] + e - first + 1)
                    V.scalar_tensor_tensor(acc[:, slot, :], Y[:, e % 4, :], gates[:, slot, e:e + 1], old,
                                           ALU.mult, ALU.add).then_inc(acc_done, 1)

            def gru_turn(i, hf, gru, experts, steps=GS):
                G = 2 * i + hf
                for s in range(steps):
                    if gru:
                        slot = GS * hf + s
                        prev = gp[:, :] if s % 4 == 0 else g8[:, slot - 1, :]
                        t1 = GS * G + (s + 1)
                        dve.wait_ge(g_tanh, t1)
                        V.scalar_tensor_tensor(gRH[:, :], gT[:, 0, :], 1.0, prev, ALU.add, ALU.mult).then_inc(g_rh, 1)
                        V.scalar_tensor_tensor(gA[:, :], gT[:, 1, :], -1.0, prev, ALU.add, ALU.mult).then_inc(g_a, 1)
                        V.tensor_scalar(zK[:, :], gT[:, 1, :], SH / 2, SH / 2, ALU.mult, ALU.add).then_inc(g_zk, 1)
                        dve.wait_ge(g_zk, t1)
                        dve.wait_ge(g_c, t1)
                        V.tensor_tensor(gB[:, :], zK[:, :], gC[:, :], ALU.mult).then_inc(g_b, 1)
                        dve.wait_ge(g_a, t1)
                        dve.wait_ge(g_b, t1)
                        keep = -SH / 2 if s % 4 == 0 else -0.5
                        new = lambda o: V.scalar_tensor_tensor(o, gA[:, :], keep, gB[:, :], ALU.mult, ALU.add)
                        new(ghi[:, slot, :]).then_inc(g_hi, 1)
                        new(g8[:, slot, :]).then_inc(g_h, 1)
                        dve.wait_ge(g_hi, t1)
                        dve.wait_ge(g_h, t1)
                        V.tensor_tensor(glo[:, slot, :], g8[:, slot, :], ghi[:, slot, :], ALU.subtract).then_inc(g_lo, 1)
                    if experts:
                        routing(G, hf, s)
                    if s in (1, 2):
                        combine(i, hf, 1 - hf, s)
                    if s in (5, 6) and experts:
                        combine(i, hf, hf, s)

            with dve.Fori(0, NG // 2) as i:
                for hf in range(2):
                    gru_turn(i, hf, True, True)
            gru_turn(NG // 2, 0, False, True)
            gru_turn(NG // 2, 1, False, False, 3)


def kernel(**inputs):
    import concourse.bacc as _bacc
    from concourse.bass_utils import run_bass_kernel_spmd as _run

    x = {k: np.asarray(v) for k, v in inputs.items()}
    wq = x["L0_attn_Wq"]
    gz, gr, gh = x["L0_cond2_Wz"], x["L0_cond2_Wr"], x["L0_cond2_Wh"]
    q = np.arange(128) % TB
    cols = np.arange(4 * TOK) // TOK
    arrays = {
        "xT": x["x"].transpose(2, 1, 0).reshape(D, T * B),
        "h0T": x["cond_1024"].T,
        "lWx": x["L0_cond_Wx"].reshape(D, 4, 128),
        "lWh": x["L0_cond_Wh"].reshape(D, 4, 128),
        "bias": np.concatenate([
            x["L0_cond_b"].reshape(4, 1, 128),
            np.stack([x["L0_cond2_br"], x["L0_cond2_bz"], x["L0_cond2_bh"], x["L0_cond2_bp"]]).reshape(4, 1, 128)], axis=1),
        "b1": x["L0_ffn_b1"].reshape(E, FC, 128).transpose(2, 0, 1),
        "b2": x["L0_ffn_b2"].reshape(1, E * D),
        "WqT": wq.transpose(2, 1, 0),
        "WkT": x["L0_attn_Wk_up"].transpose(2, 1, 0),
        "WvT": x["L0_attn_Wv_up"].transpose(2, 1, 0),
        "Wout": x["L0_attn_Wout"].transpose(1, 0, 2),
        "Wkvd": x["L0_attn_Wkv_down"],
        "gWx": np.stack([gr[:D], gz[:D], gh[:D]], axis=1),
        "gWh": np.stack([gr[D:], gz[D:], gh[D:]], axis=1),
        "gWp": x["L0_cond2_Wp"],
        "gateW": x["L0_ffn_gate_w"].T,
        "w1": x["L0_ffn_w1"].transpose(1, 0, 2),
        "w2": x["L0_ffn_w2"].reshape(E, FC, 128, D).transpose(2, 0, 1, 3),
        "ident": np.eye(128, dtype=np.float32),
        "ind": (np.arange(12)[:, None] % 4 == cols[None, :]).astype(np.float32),
        "gscale": np.array([[0.5, 0.5], [0.5, 0.5], [0.5, 1.0], [1.0, 1.0]], np.float32) * np.float32(SP),
        "mask": np.where(np.arange(TB)[None, :] > q[:, None], np.float32(NEG), np.float32(0)),
        "tri": np.broadcast_to(np.tril(np.ones((E, E), np.float32), -1), (128, E, E)),
    }
    nc = _bacc.Bacc("TRN2", target_bir_lowering=False, num_devices=1)
    given, aps = {}, {}
    for name, v in arrays.items():
        v = np.ascontiguousarray(v)
        given[f"in_{name}"] = v
        aps[name] = nc.dram_tensor(f"in_{name}", v.shape, mybir.dt.from_np(v.dtype), kind="ExternalInput").ap()
    out = nc.dram_tensor("out", ((NG + 2) * TOK, D), mybir.dt.float32, kind="ExternalOutput").ap()
    build(nc, aps, out)
    r = _run(nc, [given], core_ids=[0])
    got = r.results[0]["out"]
    return got[2 * TOK:].reshape(T, B, D).transpose(1, 0, 2)
```

```python
import numpy as np
import concourse.bass as bass
from concourse import mybir
from contextlib import ExitStack

B, T, D = 16, 128, 128
H, HD, LD = 16, 64, 32
E, F = 8, 512
GS = 8
TOK = GS * B
NG = T // GS
TB = 32
NBLK = T // TB
HQ = 128 // TB
HG = H // HQ
BQ = B // (TB // GS)
PAD = T * B
FC = F // 128
NEG = -1.0e30
SH = 256.0
SW = 256.0
SP = SH * SW


def build(nc, a, out):
    f32 = mybir.dt.float32
    f16 = mybir.dt.float16
    bf16 = mybir.dt.bfloat16
    ALU = mybir.AluOpType
    ACT = mybir.ActivationFunctionType
    AX = mybir.AxisListType
    ds = bass.ds

    ctx = ExitStack()
    with ctx:
        def sb(name, shape, dt=f32):
            return ctx.enter_context(nc.sbuf_tensor(name, shape, dt))

        def pb(name, shape, dt=f32):
            return ctx.enter_context(nc.psum_tensor(name, shape, dt))

        def sem(name):
            return ctx.enter_context(nc.semaphore(name))

        ident = sb("ident", [128, 128])
        ident16 = sb("ident16", [128, 128], bf16)
        ind32 = sb("ind32", [12, 4 * TOK])
        ind = sb("ind", [12, 4 * TOK], bf16)
        gscale = sb("gscale", [4, 2])
        mask32 = sb("mask32", [128, TB])
        cmask = sb("cmask", [128, HG, TB], bf16)
        xT = sb("xT", [128, PAD + TB * B + B])
        h0T = sb("h0T", [128, B])
        lWx = sb("lWx", [128, 4, 128])
        lWh = sb("lWh", [128, 4, 128])
        bias = sb("bias", [4, 2, 128])
        bres = sb("bres", [4, 2, 128])
        bpart = [sb(f"bpart{n}", [4, 2, 128], bf16) for n in range(3)]
        biasP = sb("biasP", [12, 2, 128], bf16)
        b1 = sb("b1", [128, E, FC])
        b2 = sb("b2", [E, D])
        b2res = sb("b2res", [E, D])
        b2part = [sb(f"b2part{n}", [E, D], bf16) for n in range(3)]
        b2P = sb("b2P", [3, E * D], bf16)
        ones3 = sb("ones3", [3, 128], bf16)
        WqT = sb("WqT", [HD, H, D])
        WkT = sb("WkT", [HD, H, LD])
        WvT = sb("WvT", [HD, H, LD])
        Wout = sb("Wout", [HD, H, D])
        Wkvd = sb("Wkvd", [128, HQ, LD])
        Wqk = sb("Wqk", [128, H, LD])
        Wvo = sb("Wvo", [128, HG, D])
        gWx = sb("gWx", [128, 3, 128])
        gWh = sb("gWh", [128, 3, 128])
        gW1 = sb("gW1", [128, 3, 128])
        gW2 = sb("gW2", [128, 3, 128])
        gWhi = sb("gWhi", [128, 2, 128], f16)
        gWlo = sb("gWlo", [128, 2, 128], f16)
        lWhi = sb("lWhi", [128, 4, 128], f16)
        lWlo = sb("lWlo", [128, 4, 128], f16)
        w1hi = sb("w1hi", [128, E, F], f16)
        w1lo = sb("w1lo", [128, E, F], f16)
        gWp = sb("gWp", [128, 128])
        gateW = sb("gateW", [128, E])
        w1 = sb("w1", [128, E, F])
        w2 = sb("w2", [128, E, FC, D])

        h16 = sb("h16", [128, 2 * GS, B])
        still = sb("still", [128, 512], bf16)
        hhi = sb("hhi", [128, B], f16)
        hlo = sb("hlo", [128, B], f16)
        oK = sb("oK", [128, B])
        lT = sb("lT", [128, 5, B])
        lP = sb("lP", [128, 2, B])
        lC = sb("lC", [128, B])
        latT = sb("latT", [128, B, GS + T])
        latS = sb("latS", [128, BQ, TB])
        latR = sb("latR", [128, BQ, LD])
        latN = sb("latN", [128, B, LD + 1])
        qT = sb("qT", [128, 2, HG, B, TB])
        qbd = sb("qbd", [128, 2, HG, HQ, TB])
        mx = sb("mx", [128, 2, HG])
        P = sb("P", [128, BQ, HG, T])
        PTs = sb("PTs", [128, 2, HG, 128])
        rs = sb("rs", [128, HG])
        On = sb("On", [128, HG, LD])
        OT = sb("OT", [128, HG, BQ, TB])
        x1T = sb("x1T", [128, TOK + PAD + TB * B + B])
        g8 = sb("g8", [128, 2 * GS + 2, B])
        gp = g8[:, 2 * GS, :]
        ghi = sb("ghi", [128, 2 * GS, B], f16)
        glo = sb("glo", [128, 2 * GS, B], f16)
        gT = sb("gT", [128, 2, B])
        gRZ = sb("gRZ", [128, 2, B])
        gA = sb("gA", [128, B])
        gC = sb("gC", [128, B])
        gB = sb("gB", [128, B])
        tri = sb("tri", [128, E, E])
        stx = sb("stx", [128, TOK])
        xn = sb("xn", [128, D])
        hidA = sb("hidA", [128, 2, TOK])
        hidB = sb("hidB", [128, 2, TOK])
        lg = sb("lg", [128, E])
        lmax = sb("lmax", [128, 1])
        low = sb("low", [128, E])
        th = sb("th", [128, E])
        eq = sb("eq", [128, E, E])
        gt = sb("gt", [128, E, E])
        rank = sb("rank", [128, E])
        den = sb("den", [128, E])
        ex = sb("ex", [128, E])
        picked = sb("picked", [128, E])
        sums = sb("sums", [128, 4])
        gates = sb("gates", [128, 2, E])
        acc = sb("acc", [128, 2, D])

        pL = [pb(f"pL{n}", [128, 4, GS, B]) for n in range(2)]
        p2 = pb("p2", [128, 512])
        p3 = pb("p3", [128, 512])
        p4 = pb("p4", [128, 512])
        p5 = pb("p5", [128, 512])
        p6 = pb("p6", [128, 512])
        p7 = pb("p7", [128, 512])
        pS = [p2, p3]
        pT, pQ, pO, pM = p4, p5, p6, p7
        pG = pL
        pHA, pHB, pY, pR = p2, p3, [p4, p5], p6

        loaded = sem("loaded")
        loaded2 = sem("loaded2")
        loaded3 = sem("loaded3")
        loaded_x = sem("loaded_x")
        stacked2 = sem("stacked2")
        set_gru = sem("set_gru")
        set_still = sem("set_still")
        set_lstm = sem("set_lstm")
        set_pool = sem("set_pool")
        set_dve = sem("set_dve")
        set_act = sem("set_act")
        fold_mm = sem("fold_mm")
        folded = sem("folded")
        split = sem("split")
        stacked = sem("stacked")
        opened = sem("opened")
        l_gates = sem("l_gates")
        l_tanh = sem("l_tanh")
        l_mul = sem("l_mul")
        l_c = sem("l_c")
        l_tc = sem("l_tc")
        l_h = sem("l_h")
        l_hi = sem("l_hi")
        l_lo = sem("l_lo")
        g_hi = sem("g_hi")
        g_lo = sem("g_lo")
        w1_split = sem("w1_split")
        lat_mm = sem("lat_mm")
        q_mm = sem("q_mm")
        lat_done = sem("lat_done")
        q_done = sem("q_done")
        lat_staged = sem("lat_staged")
        lat_turned = sem("lat_turned")
        latn_done = sem("latn_done")
        qbd_done = sem("qbd_done")
        qbd_last = sem("qbd_last")
        s_mm = sem("s_mm")
        mx_done = sem("mx_done")
        sub_done = sem("sub_done")
        exp_done = sem("exp_done")
        pt_mm = sem("pt_mm")
        pt_done = sem("pt_done")
        o_mm = sem("o_mm")
        rs_done = sem("rs_done")
        on_done = sem("on_done")
        ot_done = sem("ot_done")
        proj_mm = sem("proj_mm")
        x1_done = sem("x1_done")
        g_rz = sem("g_rz")
        g_tanh = sem("g_tanh")
        g_rh = sem("g_rh")
        g_a = sem("g_a")
        g_cand = sem("g_cand")
        g_c = sem("g_c")
        g_b = sem("g_b")
        g_h = sem("g_h")
        g_prop = sem("g_prop")
        g_p = sem("g_p")
        stx_done = sem("stx_done")
        r_mm = sem("r_mm")
        route = sem("route")
        th_done = sem("th_done")
        l1a = sem("l1a")
        l1b = sem("l1b")
        gelu_a = sem("gelu_a")
        gelu_b = sem("gelu_b")
        l2a = sem("l2a")
        l2b = sem("l2b")
        acc_done = sem("acc_done")
        stored = [sem(f"stored{n}") for n in range(2)]

        block = ctx.enter_context(nc.Block())

        def whole(t):
            return t[tuple(slice(None) for _ in t.shape)]

        LOADS = [(ident, "ident"), (ind32, "ind"), (gscale, "gscale"), (bias, "bias"), (h0T, "h0T"),
                 (lWx, "lWx"), (lWh, "lWh")]
        LOADS2 = [(WqT, "WqT"), (WkT, "WkT"), (WvT, "WvT"), (Wout, "Wout"), (mask32, "mask"), (b2, "b2")]
        LOADS3 = [(gWx, "gWx"), (gWh, "gWh"), (gWp, "gWp"), (gateW, "gateW"), (tri, "tri"), (b1, "b1"), (w1, "w1"), (w2, "w2")]
        N1 = 16 * len(LOADS)
        N2 = 16 * (len(LOADS2) + HQ)
        N3 = 16 * len(LOADS3)
        CLEARED = [P, lT, qbd, latN, OT, stx, hidA, hidB, ghi, glo, acc, gates]
        NSET = len(CLEARED) + 7
        LAST = BQ * 4 * (NBLK - 1)
        SETG = 7
        SETD = 2 + 4 + 4 + 2 + 1
        SETA = 12
        ROUTE = 18

        @block.sync
        def _(sp):
            sp.sem_inc(stored[0], 16)
            for t, name in LOADS:
                sp.dma_start(whole(t), a[name]).then_inc(loaded, 16)
            for q in range(HQ):
                sp.dma_start(Wkvd[:, q, :], a["Wkvd"]).then_inc(loaded2, 16)
            sp.wait_ge(split, 1)
            for n in range(3):
                sp.dma_start(biasP[4 * n:4 * n + 4, :, :], whole(bpart[n])).then_inc(stacked, 16)
            for t, name in LOADS3[:-2]:
                sp.dma_start(whole(t), a[name]).then_inc(loaded3, 16)
            sp.wait_ge(split, 2)
            for n in range(3):
                sp.dma_start(b2P[n:n + 1, :], whole(b2part[n])).then_inc(stacked2, 16)
            for t, name in LOADS3[-2:]:
                sp.dma_start(whole(t), a[name]).then_inc(loaded3, 16)
            with sp.Fori(0, NG // 2) as i:
                for hf in range(2):
                    sp.wait_ge(acc_done, 16 * i + (8 * hf + 5) + 1)
                    sp.dma_start(out[ds(i * (2 * TOK) + hf * TOK, TOK), :], acc[:, 1 - hf, :]).then_inc(stored[1 - hf], 16)
            for hf in range(2):
                sp.wait_ge(acc_done, 8 * (NG + hf) + 5 + 1)
                sp.dma_start(out[(NG + hf) * TOK:(NG + hf + 1) * TOK, :], acc[:, 1 - hf, :]).then_inc(stored[1 - hf], 16)
            for n in range(2):
                sp.wait_ge(stored[n], 16 * (NG // 2 + 2 - n))

        @block.gpsimd
        def _(pool):
            pool.sem_inc(latn_done, 1)
            for t in CLEARED:
                pool.memset(whole(t), 0.0).then_inc(set_pool, 1)
            pool.memset(xT[:, PAD:], 0.0).then_inc(set_pool, 1)
            pool.memset(x1T[:, 0:TOK], 0.0).then_inc(set_pool, 1)
            pool.memset(x1T[:, TOK + PAD:], 0.0).then_inc(set_pool, 1)
            pool.memset(g8[:, 0:2 * GS, :], 0.0).then_inc(set_pool, 1)
            pool.memset(g8[:, 2 * GS + 1, :], SH / 2).then_inc(set_pool, 1)
            pool.memset(whole(ones3), 1.0).then_inc(set_pool, 1)
            pool.wait_ge(set_pool, NSET - 1)
            pool.memset(latN[:, :, LD:LD + 1], 1.0).then_inc(set_pool, 1)
            pool.wait_ge(loaded3, N3)
            pool.tensor_scalar(whole(w1hi), whole(w1), SW, None, ALU.mult).then_inc(w1_split, 1)
            pool.tensor_scalar(whole(w1), whole(w1), SW, None, ALU.mult).then_inc(w1_split, 1)
            pool.wait_ge(w1_split, 2)
            pool.tensor_tensor(whole(w1lo), whole(w1), whole(w1hi), ALU.subtract).then_inc(w1_split, 1)
            pool.wait_ge(w1_split, 3)
            for j in range(NBLK):
                rows = slice(TB * j, TB * (j + 1))
                with pool.Fori(0, 2) as i:
                    for hf in range(2):
                        turn = 2 * i + (4 * j + hf)
                        b0 = 2 * BQ * i + BQ * hf
                        pool.wait_ge(lat_done, 4 * (j + 1) + 1 + 1)
                        pool.wait_ge(lat_turned, turn + 1)
                        pool.tensor_copy(latS[rows, :, :],
                                         latT[rows, ds(b0, BQ), GS + TB * j:GS + TB * (j + 1)]).then_inc(lat_staged, 1)
                        pool.wait_ge(q_done, 4 * (j + 1) + 1 + 1)
                        for k in range(BQ):
                            if k == 2:
                                pool.wait_ge(lat_turned, turn + 1 + 1)
                                pool.tensor_copy(latN[rows, ds(b0, BQ), 0:LD], latR[rows, :, :]).then_inc(latn_done, 1)
                            pool.wait_ge(s_mm, BQ * turn + (k + 1))
                            for q in range(HQ - (j == NBLK - 1)):
                                r = slice(32 * q, 32 * q + 32)
                                pool.tensor_copy(qbd[r, k % 2, :, q, :], qT[r, j % 2, :, ds(b0 + k, 1), :]
                                                 .rearrange("p g o t -> p g (o t)")).then_inc(qbd_done, 1)

            def stage(G, off):
                pool.wait_ge(r_mm, 2 * G + 1)
                pool.tensor_copy(whole(stx), x1T[:, off]).then_inc(stx_done, 1)

            pool.wait_ge(x1_done, 4 * NBLK + 1)
            with pool.Fori(0, NG // 2) as i:
                for hf in range(2):
                    stage(2 * i + hf, ds(i * (2 * TOK) + hf * TOK, TOK))
            stage(NG, slice(NG * TOK, (NG + 1) * TOK))

        @block.tensor
        def _(pe):
            def mm(out, lhsT, rhs, start=False, stop=True):
                return nc.tensor.matmul(out, lhsT=lhsT, rhs=rhs, start=start, stop=stop, skip_group_check=True)

            def flat(t):
                return t.rearrange("p a b -> p (a b)")

            def keep_warm(n):
                for _ in range(n):
                    mm(pM[:, :], still[:, 0:128], still[:, :], start=True)

            pe.sem_inc(s_mm, 2)
            pe.sem_inc(pt_mm, BQ)
            for x in (r_mm, l1a, l1b, l2a, l2b):
                pe.sem_inc(x, 1)
            pe.wait_ge(set_still, 2)
            keep_warm(12)
            pe.wait_ge(loaded2, N2)
            for h in range(H):
                mm(p2[:, LD * h:LD * (h + 1)], WqT[:, h, :], WkT[:, h, :], start=True)
            for h in range(H):
                q, g = h % HQ, h // HQ
                last = mm(p3[32 * q:32 * q + 32, D * g:D * (g + 1)], WvT[:, h, :], Wout[:, h, :], start=True)
            last.then_inc(fold_mm, 1)
            pe.wait_ge(set_pool, NSET)
            pe.wait_ge(set_dve, SETD)
            pe.wait_ge(set_act, SETA)
            pe.wait_ge(stacked, 16 * 3)
            pe.wait_ge(loaded_x, 16)

            def l_fill(G, hf, g):
                if g == 0:
                    mm(pL[hf][:, :, :, :].rearrange("p g s b -> p (g s b)"), biasP[:, 0, :], ind[:, :], start=True)
                return mm(pL[hf][:, g, :, :].rearrange("p s b -> p (s b)"), lWx[:, g, :], xT[:, ds(G * TOK, TOK)])

            for g in range(4):
                l_fill(0, 0, g)

            def lat_q(turn, hf):
                src = h16[:, GS * (1 - hf):GS * (2 - hf), :].rearrange("p s b -> p (s b)")
                pe.wait_ge(l_h, GS * turn + 1)
                pe.wait_ge(lat_done, turn + 1)
                pe.wait_ge(q_done, turn + 1)
                mm(pM[:, 0:TOK], flat(Wkvd[:, :, :]), src, start=True).then_inc(lat_mm, 1)
                for g in range(HG):
                    last = mm(pQ[:, TOK * g:TOK * (g + 1)], flat(Wqk[:, HQ * g:HQ * (g + 1), :]), src, start=True)
                last.then_inc(q_mm, 1)

            def project(turn, bank=pO):
                pe.wait_ge(ot_done, BQ * turn + 1)
                if bank is pM:
                    pe.wait_ge(x1_done, turn)
                for g in range(HG):
                    last = mm(bank[:, 256:256 + TOK], Wvo[:, g, :], flat(OT[:, g, :, :]), start=(g == 0))
                last.then_inc(proj_mm, 1)

            def scores(n, k, L, b, last_block=False):
                if last_block:
                    pe.wait_ge(qbd_done, 3 * n + (LAST + 3))
                    pe.wait_ge(qbd_last, n - (LAST - 1))
                else:
                    pe.wait_ge(qbd_done, 4 * n + 4)
                pe.wait_ge(sub_done, n + 1)
                S = pS[k % 2]
                mm(S[:, :].rearrange("p (g t) -> p g t", g=HG)[:, :, L - TB:L], ident16[:, :],
                   cmask[:, :, :], start=True)
                for g in range(HG):
                    last = mm(S[:, T * g:T * g + L], flat(qbd[:, k % 2, g, :, :]),
                              latT[:, ds(b, 1), GS:GS + L].rearrange("p o t -> p (o t)"))
                last.then_inc(s_mm, 1)

            def turn_probs(n, k, L):
                pe.wait_ge(exp_done, n + 1)
                pe.wait_ge(pt_done, n + 1)
                for g in range(HG):
                    last = nc.tensor.transpose(pT[:, 128 * g:128 * (g + 1)], P[:, k, g, :], ident[:, :])
                last.then_inc(pt_mm, 1)

            def values(n, k, L, b, turn, last_block=False):
                pe.wait_ge(pt_done, n + 1 + 1)
                if k == 0:
                    pe.wait_ge(latn_done, turn + 1 + 1)
                    if not last_block:
                        pe.wait_ge(x1_done, turn + 1)
                pe.wait_ge(on_done, n + 1)
                for g in range(HG):
                    last = mm(pO[:, (LD + 1) * g:(LD + 1) * (g + 1)], PTs[0:L, k % 2, g, :],
                              latN[0:L, ds(b, 1), :].rearrange("p o c -> p (o c)"), start=(g == 0))
                last.then_inc(o_mm, 1)

            def attention(s, turn, L, b0):
                if s == 0:
                    project(turn)
                if 1 <= s <= 4:
                    scores(BQ * turn + (s - 1), s - 1, L, b0 + (s - 1))
                if 4 <= s <= 7:
                    values(BQ * turn + (s - 4), s - 4, L, b0 + (s - 4), turn)
                if 3 <= s <= 6:
                    turn_probs(BQ * turn + (s - 3), s - 3, L)

            WARM = [[0, 4, 4, 5, 5, 4, 4, 5]] + [[0, 4, 3, 3, 2, 2, 2, 4]] * 3
            for p in range(NBLK):
                with pe.Fori(0, 2) as i:
                    for hf in range(2):
                        G = 2 * i + (4 * p + hf)
                        for s in range(GS):
                            pe.wait_ge(l_hi, GS * G + (s + 1))
                            for g in range(4):
                                mm(pL[hf][:, g, s, :], lWhi[:, g, :], hhi[:, :])
                                mm(pL[hf][:, g, s, :], lWlo[:, g, :], hhi[:, :])
                            pe.wait_ge(l_lo, GS * G + (s + 1))
                            for g in range(4):
                                last = mm(pL[hf][:, g, s, :], lWhi[:, g, :], hlo[:, :])
                            last.then_inc(l_gates, 1)
                            if s == 1:
                                pe.wait_ge(lat_done, G + 2)
                            if s > 0:
                                keep_warm(WARM[p][s])
                            if s == 0:
                                lat_q(G, hf)
                            if s in (1, 2, 5, 6):
                                l_fill(G + 1, 1 - hf, (1, 2, 5, 6).index(s))
                            if p > 0:
                                attention(s, G - 4, TB * p, 2 * BQ * i + BQ * hf)

            def last_attention(i, first, slots=BQ):
                for k in range(slots):
                    n = 4 * i + (LAST + k)
                    if slots == BQ:
                        scores(n, k, T, 4 * i + k, True)
                    else:
                        k += BQ
                    if slots < BQ and k == BQ or slots == BQ and not (first and k == 0):
                        turn_probs(n - 1, (k - 1) % BQ, T)
                    for _ in range(WARM_LAST):
                        mm(pQ[:, :], still[:, 0:128], still[:, :], start=True)
                    if slots == BQ and k == 2:
                        project(i + 4 * (NBLK - 1), pM)
                    if not (first and k < 2):
                        values(n - 2, (k - 2) % BQ, T, 4 * i + (k % BQ if slots < BQ else k) - 2, i + 4 * (NBLK - 1), True)

            WARM_LAST = 1
            lat_q(4 * NBLK, 0)
            pe.wait_ge(lat_done, 4 * NBLK + 1 + 1)
            pe.wait_ge(q_done, 4 * NBLK + 1 + 1)
            last_attention(0, True)
            with pe.Fori(1, 4) as i:
                last_attention(i, False)
            last_attention(4, False, 2)
            project(4 * NBLK, pM)

            def g_fill(G, hf, g):
                if g == 0:
                    mm(pG[hf][:, :, :, :].rearrange("p g s b -> p (g s b)"), biasP[:, 1, :], ind[:, :], start=True)
                return mm(pG[hf][:, g, :, :].rearrange("p s b -> p (s b)"), gWx[:, g, :], x1T[:, ds(G * TOK + TOK, TOK)])

            pe.wait_ge(x1_done, 4 * NBLK + 1)
            pe.wait_ge(set_gru, SETG + 1)
            pe.wait_ge(stacked2, 16 * 3)
            for g in range(3):
                g_fill(0, 0, g)
            mm(pY[1][:, :], ones3[:, :], b2P[:, 512:1024], start=True)
            mm(pHB[:, 0:2 * TOK], biasP[:, 1, :], ind[:, 0:2 * TOK], start=True).then_inc(opened, 1)
            pe.wait_ge(w1_split, 3)

            def route_x(G, hf):
                pe.wait_ge(route, ROUTE * G + 1)
                pe.wait_ge(stx_done, G + 1)
                mm(pR[:, 0:E], g8[:, GS * (1 - hf):GS * (2 - hf), :].rearrange("p s b -> p (s b)"), gateW[:, :],
                   start=True).then_inc(r_mm, 1)
                nc.tensor.transpose(pR[:, 128:256], stx[:, :], ident[:, :]).then_inc(r_mm, 1)

            def layer1(G, hf, e, half):
                bank, free, done = ((pHA, gelu_a, l1a), (pHB, gelu_b, l1b))[half]
                pe.wait_ge(free, E * G + (e + half) + 1)
                hi, lo = (t[:, GS * (1 - hf):GS * (2 - hf), :].rearrange("p s b -> p (s b)") for t in (ghi, glo))
                for c in range(2):
                    Y, cols = bank[:, TOK * c:TOK * (c + 1)], slice(128 * (2 * half + c), 128 * (2 * half + c + 1))
                    mm(Y, w1hi[:, e, cols], hi, start=(c == 0))
                    mm(Y, w1hi[:, e, cols], lo)
                    last = mm(Y, w1lo[:, e, cols], hi)
                last.then_inc(done, 1)

            def layer2(G, e, half, chunks=(0, 1)):
                hid, ready, done = ((hidA, gelu_a, l2a), (hidB, gelu_b, l2b))[half]
                Y = pY[e // 4]
                if half == 0 and e % 4 == 0 and 0 in chunks:
                    pe.wait_ge(acc_done, 8 * G + (e + 1) + 1)
                    mm(Y[:, :], ones3[:, :], b2P[:, 512 * (e // 4):512 * (e // 4) + 512], start=True)
                if 0 in chunks:
                    pe.wait_ge(ready, E * G + ((e + 1) % E + half) + 1)
                for c in chunks:
                    last = mm(Y[:, D * (e % 4):D * (e % 4 + 1)], hid[:, c, :], w2[:, e, 2 * half + c, :])
                if c == 1:
                    last.then_inc(done, 1)

            def gru_turn(i, hf, gru, experts, steps=GS):
                G = 2 * i + hf
                for s in range(steps):
                    if gru:
                        if s % 4 == 0:
                            pe.wait_ge(g_p, 2 * G + (s // 4 + 1))
                            W = gW1
                            for g in range(2):
                                last = mm(pG[hf][:, g, s, :], W[:, g, :], gp)
                        else:
                            W = gW2
                            pe.wait_ge(g_hi, GS * G + s)
                            for g in range(2):
                                mm(pG[hf][:, g, s, :], gWhi[:, g, :], ghi[:, GS * hf + s - 1, :])
                                mm(pG[hf][:, g, s, :], gWlo[:, g, :], ghi[:, GS * hf + s - 1, :])
                            pe.wait_ge(g_lo, GS * G + (s + 1))
                            for g in range(2):
                                last = mm(pG[hf][:, g, s, :], gWhi[:, g, :], glo[:, GS * hf + s - 1, :])
                        last.then_inc(g_rz, 1)
                    if experts and s == 0:
                        pe.wait_ge(g_lo, GS * G + 1)
                    if s == 0 and experts:
                        route_x(G, hf)
                    if experts:
                        layer1(G, hf, s, 0)
                    layer2(G, (s - 1) % E, 0, (0,))
                    if gru:
                        pe.wait_ge(g_rh, GS * G + (s + 1))
                        mm(pG[hf][:, 2, s, :], W[:, 2, :], gRZ[:, 0, :]).then_inc(g_cand, 1)
                    layer2(G, (s - 1) % E, 0, (1,))
                    if experts:
                        layer1(G, hf, s, 1)
                    layer2(G, (s - 1) % E, 1)
                    if gru:
                        if s in (0, 1, 2):
                            g_fill(G + 1, 1 - hf, s)
                        if s % 4 == 3:
                            pe.wait_ge(g_h, GS * G + (s + 1))
                            mm(pG[hf][:, 3, s, :], gWp[:, :], g8[:, GS * hf + s, :]).then_inc(g_prop, 1)

            with pe.Fori(0, NG // 2) as i:
                for hf in range(2):
                    gru_turn(i, hf, True, True)
            gru_turn(NG // 2, 0, False, True)
            gru_turn(NG // 2, 1, False, False, 1)

        @block.scalar
        def _(act):
            A = nc.scalar.activation
            for t, name in LOADS2:
                act.dma_start(whole(t), a[name]).then_inc(loaded2, 16)
            act.dma_start(xT[:, 0:PAD], a["xT"]).then_inc(loaded_x, 16)
            for x in (q_done, pt_done, gelu_a, gelu_b):
                act.sem_inc(x, 1)
            act.wait_ge(loaded, N1)
            A(h16[:, 2 * GS - 1, :], h0T[:, :], ACT.Copy, scale=SH).then_inc(set_act, 1)
            A(hhi[:, :], h0T[:, :], ACT.Copy, scale=SH).then_inc(set_act, 1)
            A(ident16[:, :], ident[:, :], ACT.Copy).then_inc(set_act, 1)
            A(ind[:, :], ind32[:, :], ACT.Copy).then_inc(set_act, 1)
            A(lWh[:, 0:3, :], lWh[:, 0:3, :], ACT.Copy, scale=0.5 * SW).then_inc(set_act, 1)
            A(lWh[:, 3, :], lWh[:, 3, :], ACT.Copy, scale=SW).then_inc(set_act, 1)
            act.wait_ge(set_act, 6)
            A(lWhi[:, :, :], lWh[:, :, :], ACT.Copy).then_inc(set_act, 1)
            A(lWx[:, 0:3, :], lWx[:, 0:3, :], ACT.Copy, scale=0.5 * SP).then_inc(set_act, 1)
            A(lWx[:, 3, :], lWx[:, 3, :], ACT.Copy, scale=SP).then_inc(set_act, 1)
            act.wait_ge(loaded2, N2)
            A(Wkvd[:, :, :], Wkvd[:, :, :], ACT.Copy, scale=1.0 / SH).then_inc(set_act, 1)
            act.wait_ge(fold_mm, 1)
            A(Wqk[:, :, :].rearrange("p h c -> p (h c)"), p2[:, :], ACT.Copy, scale=1.0 / SH / HD ** 0.5).then_inc(set_act, 1)
            A(Wvo[:, :, :].rearrange("p g d -> p (g d)"), p3[:, :], ACT.Copy).then_inc(set_act, 1)

            def q_copy(turn, par, t0):
                act.wait_ge(q_mm, turn + 1)
                A(qT[:, ds(par, 1), :, :, ds(t0, GS)].rearrange("p o g b t -> p (o g) b t"), pQ[:, :].rearrange("p (g s b) -> p g b s", g=HG, b=B),
                  ACT.Copy).then_inc(q_done, 1)

            def exps(n, k, L):
                act.wait_ge(sub_done, n + 3)
                A(P[:, k, :, 0:L], P[:, k, :, 0:L], ACT.Exp).then_inc(exp_done, 1)

            def pt_copy(n, k, L):
                act.wait_ge(pt_mm, n + (BQ + 1))
                A(PTs[0:L, k % 2, :, :].rearrange("p g q -> p (g q)"), pT[0:L, :], ACT.Copy).then_inc(pt_done, 1)

            def last_query(n, k, b):
                act.wait_ge(s_mm, n + 1)
                r = slice(128 - 32, 128)
                A(qbd[r, k % 2, :, HQ - 1, :], qT[r, (NBLK - 1) % 2, :, ds(b, 1), :]
                  .rearrange("p g o t -> p g (o t)"), ACT.Copy).then_inc(qbd_last, 1)

            def last_attention(i, first, last):
                for k in range(BQ):
                    n = 4 * i + (LAST + k)
                    if not (first and k == 0):
                        exps(n - 1, (k - 1) % BQ, T)
                    if not (last and k == BQ - 1):
                        last_query(n + 1, k + 1, 4 * i + k + 1)
                    if not (first and k == 0):
                        pt_copy(n - 1, (k - 1) % BQ, T)

            for p in range(NBLK):
                with act.Fori(0, 2) as i:
                    for hf in range(2):
                        G = 2 * i + (4 * p + hf)
                        turn = 2 * i + (4 * p + hf - 4)
                        for s in range(GS):
                            act.wait_ge(l_gates, GS * G + (s + 1))
                            A(lT[:, 0:4, :], pL[hf][:, :, s, :], ACT.Tanh, scale=1.0 / SP).then_inc(l_tanh, 1)
                            act.wait_ge(l_c, GS * G + (s + 1))
                            A(lC[:, :], lT[:, 4, :], ACT.Tanh, scale=0.5).then_inc(l_tc, 1)
                            if s == 0 and hf == 0:
                                was, now = (p - 1) % 2, p % 2
                                q_copy(G, i * (now - was) + was, i * (GS - (TB - GS)) + (TB - GS))
                            if s == 0 and hf == 1:
                                q_copy(G, p % 2, 2 * GS * i)
                            if p > 0:
                                L = TB * p
                                if 2 <= s <= 5:
                                    exps(BQ * turn + (s - 2), s - 2, L)
                                if 3 <= s <= 6:
                                    pt_copy(BQ * turn + (s - 3), s - 3, L)
            q_copy(4 * NBLK, (NBLK - 1) % 2, TB - GS)
            act.wait_ge(q_done, 4 * NBLK + 1 + 1)
            last_query(LAST, 0, 0)
            last_attention(0, True, False)
            with act.Fori(1, 3) as i:
                last_attention(i, False, False)
            last_attention(3, False, True)
            exps(LAST + B - 1, BQ - 1, T)
            pt_copy(LAST + B - 1, BQ - 1, T)
            act.wait_ge(loaded3, N3)
            A(gW1[:, :, :], gWh[:, :, :], ACT.Copy, scale=0.5 * SP).then_inc(set_gru, 1)
            A(gW2[:, :, :], gWh[:, :, :], ACT.Copy, scale=0.5 * SW).then_inc(set_gru, 1)
            A(gWhi[:, :, :], gWh[:, 0:2, :], ACT.Copy, scale=0.5 * SW).then_inc(set_gru, 1)
            A(gWx[:, 0:2, :], gWx[:, 0:2, :], ACT.Copy, scale=0.5 * SP).then_inc(set_gru, 1)
            A(gWx[:, 2, :], gWx[:, 2, :], ACT.Copy, scale=SP).then_inc(set_gru, 1)
            A(gWp[:, :], gWp[:, :], ACT.Copy, scale=SW).then_inc(set_gru, 1)
            A(gateW[:, :], gateW[:, :], ACT.Copy, scale=1.0 / SH).then_inc(set_gru, 1)
            A(gp, h0T[:, :], ACT.Copy).then_inc(g_p, 1)

            def gelu(n, e, half, step):
                bank, hid, full, read, done = ((pHA, hidA, l1a, l2a, gelu_a), (pHB, hidB, l1b, l2b, gelu_b))[half]
                act.wait_ge(full, n + 1)
                act.wait_ge(read, step + 1)
                for c in range(2):
                    last = A(hid[:, c, :], bank[:, TOK * c:TOK * (c + 1)], ACT.Gelu,
                             bias=b1[:, e, 2 * half + c:2 * half + c + 1], scale=1.0 / SP)
                last.then_inc(done, 1)

            def gru_turn(i, hf, gru, experts, steps=GS):
                G = 2 * i + hf
                for s in range(steps):
                    if gru:
                        act.wait_ge(g_rz, GS * G + (s + 1))
                        A(gT[:, :, :], pG[hf][:, 0:2, s, :], ACT.Tanh, scale=1.0 / SP).then_inc(g_tanh, 1)
                    gelu(E * G + s, (s - 1) % E, 1, E * G + s)
                    if s == 2 and experts:
                        act.wait_ge(route, ROUTE * G + 4 + 1)
                        A(th[:, :], low[:, :], ACT.Tanh, scale=0.5).then_inc(th_done, 1)
                    if gru:
                        act.wait_ge(g_cand, GS * G + (s + 1))
                        A(gC[:, :], pG[hf][:, 2, s, :], ACT.Tanh, scale=1.0 / SP).then_inc(g_c, 1)
                    if experts:
                        gelu(E * G + (s + 1), s, 0, E * G + (s + 1))
                    if gru and s % 4 == 3:
                        act.wait_ge(g_prop, 2 * G + (s // 4 + 1))
                        A(gp, pG[hf][:, 3, s, :], ACT.Tanh, scale=1.0 / SP).then_inc(g_p, 1)

            A(th[:, :], still[:, 0:E], ACT.Gelu)
            act.wait_ge(opened, 1)
            with act.Fori(0, NG // 2) as i:
                for hf in range(2):
                    gru_turn(i, hf, True, True)
            gru_turn(NG // 2, 0, False, True)
            gru_turn(NG // 2, 1, False, False, 1)

        @block.vector
        def _(dve):
            V = nc.vector
            dve.sem_inc(sub_done, 2)
            for x in (lat_turned, lat_done, ot_done, on_done, acc_done, route):
                dve.sem_inc(x, 1)
            steps = [0]

            def link(ins):
                steps[0] += 1
                ins.then_inc(set_dve, 1)
                dve.wait_ge(set_dve, steps[0])

            def split3(x, res, parts):
                link(V.tensor_copy(whole(parts[0]), whole(x)))
                link(V.tensor_tensor(whole(res), whole(x), whole(parts[0]), ALU.subtract))
                link(V.tensor_copy(whole(parts[1]), whole(res)))
                link(V.tensor_tensor(whole(res), whole(res), whole(parts[1]), ALU.subtract))
                V.tensor_copy(whole(parts[2]), whole(res)).then_inc(split, 1)

            V.memset(whole(still), 0.0).then_inc(set_still, 1)
            V.memset(h16[:, 0:2 * GS - 1, :], 0.0).then_inc(set_still, 1)
            dve.wait_ge(loaded, N1)
            for n in range(2):
                link(V.tensor_scalar(bias[:, n, :], bias[:, n, :], gscale[:, n:n + 1], None, ALU.mult))
            split3(bias, bres, bpart)
            dve.wait_ge(set_act, 7)
            link(V.tensor_tensor(lWlo[:, :, :], lWh[:, :, :], lWhi[:, :, :], ALU.subtract))
            link(V.tensor_tensor(hlo[:, :], h16[:, 2 * GS - 1, :], hhi[:, :], ALU.subtract))
            dve.wait_ge(loaded2, N2)
            split3(b2, b2res, b2part)
            link(V.tensor_copy(cmask[:, :, :], mask32[:, :].unsqueeze(1).to_broadcast([128, HG, TB])))
            for x in (l_hi, l_lo, l_h, g_lo):
                dve.sem_inc(x, 1)
            assert steps[0] == SETD
            dve.wait_ge(set_pool, NSET)

            def lat_copy(n):
                dve.wait_ge(lat_mm, n + 1)
                V.tensor_copy(latT[:, :, ds(n * GS, GS)],
                              pM[:, 0:TOK].rearrange("p (s b) -> p b s", b=B)).then_inc(lat_done, 1)

            def add_x(turn, off, bank=pO):
                dve.wait_ge(proj_mm, turn + 1)
                V.tensor_tensor(x1T[:, ds(off + TOK, TB * B)].rearrange("p (t b) -> p b t", b=B)[:, 0:BQ, :],
                                bank[:, 256:256 + TOK].rearrange("p (b t) -> p b t", b=BQ),
                                xT[:, ds(off, TB * B)].rearrange("p (t b) -> p b t", b=B)[:, 0:BQ, :],
                                ALU.add).then_inc(x1_done, 1)

            def S_of(k, L):
                return pS[k % 2][:, :].rearrange("p (g t) -> p g t", g=HG)[:, :, 0:L]

            def maximum(n, k, L):
                dve.wait_ge(s_mm, n + 3)
                V.tensor_reduce(mx[:, k % 2, :], S_of(k, L), AX.X, ALU.max).then_inc(mx_done, 1)

            def subtract(n, k, L):
                dve.wait_ge(mx_done, n + 1)
                dve.wait_ge(pt_mm, n + 1)
                V.tensor_tensor(P[:, k, :, 0:L], S_of(k, L),
                                mx[:, k % 2, :].unsqueeze(2).to_broadcast([128, HG, L]), ALU.subtract).then_inc(sub_done, 1)

            O = pO[:, 0:HG * (LD + 1)].rearrange("p (g c) -> p g c", g=HG)

            def normaliser(n):
                dve.wait_ge(o_mm, n + 1)
                V.reciprocal(rs[:, :].unsqueeze(2), O[:, :, LD:LD + 1]).then_inc(rs_done, 1)

            def normalise(n):
                dve.wait_ge(rs_done, n + 1)
                V.tensor_tensor(On[:, :, :], O[:, :, 0:LD], rs[:, :].unsqueeze(2).to_broadcast([128, HG, LD]),
                                ALU.mult).then_inc(on_done, 1)

            def turn_values(n, k, turn):
                dve.wait_ge(on_done, n + 1 + 1)
                if k == 0:
                    dve.wait_ge(proj_mm, turn + 1)
                V.transpose(OT[:, :, k, :], On[:, :, :]).then_inc(ot_done, 1)

            def turn_latents(turn, rows):
                dve.wait_ge(lat_staged, turn + 1)
                dve.wait_ge(latn_done, turn + 1)
                V.transpose(latR[rows, :, :], latS[rows, :, :]).then_inc(lat_turned, 1)

            for p in range(NBLK):
                rows = slice(TB * (p - 1), TB * p)
                with dve.Fori(0, 2) as i:
                    for hf in range(2):
                        G = 2 * i + (4 * p + hf)
                        turn = 2 * i + (4 * p + hf - 4)
                        for s in range(GS):
                            slot = GS * hf + s
                            dve.wait_ge(l_tanh, GS * G + (s + 1))
                            V.scalar_tensor_tensor(lP[:, :, :], lT[:, 0:2, :], 1.0, lT[:, 3:5, :], ALU.add, ALU.mult).then_inc(l_mul, 1)
                            V.tensor_scalar(oK[:, :], lT[:, 2, :], SH / 2, SH / 2, ALU.mult, ALU.add)
                            dve.wait_ge(l_mul, GS * G + (s + 1))
                            V.scalar_tensor_tensor(lT[:, 4, :], lP[:, 1, :], 0.5, lP[:, 0, :], ALU.mult, ALU.add).then_inc(l_c, 1)
                            if p > 0 and s >= 4:
                                normaliser(BQ * turn + (s - 4))
                            dve.wait_ge(l_tc, GS * G + (s + 1))
                            V.tensor_tensor(hhi[:, :], oK[:, :], lC[:, :], ALU.mult).then_inc(l_hi, 1)
                            V.tensor_tensor(h16[:, slot, :], oK[:, :], lC[:, :], ALU.mult).then_inc(l_h, 1)
                            dve.wait_ge(l_h, GS * G + (s + 2))
                            V.tensor_tensor(hlo[:, :], h16[:, slot, :], hhi[:, :], ALU.subtract).then_inc(l_lo, 1)
                            if s == 0:
                                lat_copy(G)
                            if p > 0:
                                L = TB * p
                                if s == 0:
                                    if hf == 0:
                                        was = TB * B * (p - 2 if p > 1 else NBLK) + 3 * BQ
                                        now = TB * B * (p - 1) + BQ
                                        add_x(turn, i * (now - was) + was)
                                    else:
                                        add_x(turn, i * (2 * BQ) + TB * B * (p - 1))
                                    turn_latents(turn, rows)
                                n, m = BQ * turn + (s - 1), BQ * turn + (s - 4)
                                if s >= 4:
                                    normalise(m)
                                if 1 <= s <= 4:
                                    maximum(n, s - 1, L)
                                if s >= 4:
                                    turn_values(m, s - 4, turn)
                                if 1 <= s <= 4:
                                    subtract(n, s - 1, L)

            def last_attention(i, first, slots=BQ):
                turn = i + 4 * (NBLK - 1)
                off = TB * B * (NBLK - 1)
                for k in range(slots):
                    n = 4 * i + (LAST + k)
                    if slots == BQ and k == 0:
                        turn_latents(turn, slice(TB * (NBLK - 1), TB * NBLK))
                    if slots == BQ and k == 3:
                        add_x(turn, off - TB * B + 3 * BQ if first else 4 * i + (off - BQ), pM)
                    if not (first and k < 3):
                        normaliser(n - 3)
                        normalise(n - 3)
                        turn_values(n - 3, (k - 3) % BQ, turn)
                    if slots == BQ:
                        maximum(n, k, T)
                        subtract(n, k, T)

            lat_copy(4 * NBLK)
            last_attention(0, True)
            with dve.Fori(1, 4) as i:
                last_attention(i, False)
            last_attention(4, False, 3)
            add_x(4 * NBLK, TB * B * (NBLK - 1) + 3 * BQ, pM)
            dve.wait_ge(set_gru, SETG)
            V.tensor_tensor(gWlo[:, :, :], gW2[:, 0:2, :], gWhi[:, :, :], ALU.subtract).then_inc(set_gru, 1)

            def routing(G, hf, s, late):
                li, lj = lg[:, :].unsqueeze(2).to_broadcast([128, E, E]), lg[:, :].unsqueeze(1).to_broadcast([128, E, E])
                ops = [
                    (0, 1, lambda: V.tensor_copy(lg[:, :], pR[:, 0:E])),
                    (0, 1, lambda: V.tensor_copy(xn[:, :], pR[:, 128:256])),
                    (0, 1, lambda: V.tensor_reduce(lmax[:, :], lg[:, :], AX.X, ALU.max)),
                    (1, 0, lambda: V.tensor_scalar(low[:, :], lg[:, :], lmax[:, 0:1], None, ALU.subtract)),
                    (1, 1, lambda: V.tensor_tensor(eq[:, :, :], lj, li, ALU.is_equal)),
                    (1, 1, lambda: V.tensor_tensor(gt[:, :, :], lj, li, ALU.is_gt)),
                    (2, 0, lambda: V.tensor_tensor(eq[:, :, :], eq[:, :, :], tri[:, :, :], ALU.mult)),
                    (2, 1, lambda: V.tensor_tensor(gt[:, :, :], gt[:, :, :], eq[:, :, :], ALU.add)),
                    (2, 1, lambda: V.tensor_reduce(rank[:, :], gt[:, :, :], AX.X, ALU.add)),
                    (3, 0, lambda: V.tensor_scalar(den[:, :], th[:, :], -1.0, 1.0, ALU.mult, ALU.add)),
                    (3, 1, lambda: V.reciprocal(den[:, :], den[:, :])),
                    (3, 1, lambda: V.scalar_tensor_tensor(ex[:, :], th[:, :], 1.0, den[:, :], ALU.add, ALU.mult)),
                    (4, 0, lambda: V.tensor_reduce(sums[:, 0:1], ex[:, :], AX.X, ALU.add)),
                    (4, 1, lambda: V.scalar_tensor_tensor(picked[:, :], rank[:, :], 2.0, ex[:, :], ALU.is_lt, ALU.mult)),
                    (4, 1, lambda: V.tensor_reduce(sums[:, 1:2], picked[:, :], AX.X, ALU.add)),
                    (4, 1, lambda: V.scalar_tensor_tensor(sums[:, 2:3], sums[:, 0:1], 1.0e-9, sums[:, 1:2], ALU.mult, ALU.add)),
                    (5, 0, lambda: V.reciprocal(sums[:, 3:4], sums[:, 2:3])),
                    (5, 0, lambda: V.tensor_scalar(gates[:, hf, :], picked[:, :], sums[:, 3:4], None, ALU.mult)),
                ]
                assert len(ops) == ROUTE
                for at, (step, when, op) in enumerate(ops):
                    if (step, when) != (s, late):
                        continue
                    if at == 0:
                        dve.wait_ge(r_mm, 2 * G + 2 + 1)
                    if at == 9:
                        dve.wait_ge(th_done, G + 1)
                    dve.wait_ge(route, ROUTE * G + at + 1)
                    op().then_inc(route, 1)

            def combine(i, hf, slot, s):
                G = 2 * i + hf
                e = (s - 5) % E
                Y = pY[e // 4][:, :].rearrange("p (e d) -> p e d", e=4)
                if s in (1, 5):
                    dve.wait_ge(l2b, E * G + {1: 2, 5: 6}[s])
                if s == 5:
                    dve.wait_ge(stored[hf], 16 * i + 16)
                    dve.wait_ge(route, ROUTE * G + ROUTE + 1)
                old = xn[:, :] if e == 0 else acc[:, slot, :]
                dve.wait_ge(acc_done, 8 * G + (s + 1))
                V.scalar_tensor_tensor(acc[:, slot, :], Y[:, e % 4, :], gates[:, slot, e:e + 1], old,
                                       ALU.mult, ALU.add).then_inc(acc_done, 1)

            def gru_turn(i, hf, gru, experts, steps=GS):
                G = 2 * i + hf
                for s in range(steps):
                    if gru:
                        slot = GS * hf + s
                        at = 2 * GS if s % 4 == 0 else slot - 1
                        prev, last = g8[:, at, :], 2 * GS + 1
                        t1 = GS * G + (s + 1)
                        dve.wait_ge(g_tanh, t1)
                        V.scalar_tensor_tensor(gRZ[:, :, :], gT[:, :, :], 1.0, g8[:, at:last + 1:last - at, :],
                                               ALU.add, ALU.mult).then_inc(g_rh, 1)
                        V.scalar_tensor_tensor(gA[:, :], gT[:, 1, :], -1.0, prev, ALU.add, ALU.mult).then_inc(g_a, 1)
                    if experts:
                        routing(G, hf, s, 0)
                    if s < 5:
                        combine(i, hf, 1 - hf, s)
                    elif experts:
                        combine(i, hf, hf, s)
                    if gru:
                        dve.wait_ge(g_c, t1)
                        V.tensor_tensor(gB[:, :], gRZ[:, 1, :], gC[:, :], ALU.mult).then_inc(g_b, 1)
                        dve.wait_ge(g_b, t1)
                        keep = -SH / 2 if s % 4 == 0 else -0.5
                        new = lambda o: V.scalar_tensor_tensor(o, gA[:, :], keep, gB[:, :], ALU.mult, ALU.add)
                        new(ghi[:, slot, :]).then_inc(g_hi, 1)
                        new(g8[:, slot, :]).then_inc(g_h, 1)
                        dve.wait_ge(g_h, t1)
                        V.tensor_tensor(glo[:, slot, :], g8[:, slot, :], ghi[:, slot, :], ALU.subtract).then_inc(g_lo, 1)
                    if experts:
                        routing(G, hf, s, 1)

            with dve.Fori(0, NG // 2) as i:
                for hf in range(2):
                    gru_turn(i, hf, True, True)
            gru_turn(NG // 2, 0, False, True)
            gru_turn(NG // 2, 1, False, False, 5)


def kernel(**inputs):
    import concourse.bacc as _bacc
    from concourse.bass_utils import run_bass_kernel_spmd as _run

    x = {k: np.asarray(v) for k, v in inputs.items()}
    wq = x["L0_attn_Wq"]
    gz, gr, gh = x["L0_cond2_Wz"], x["L0_cond2_Wr"], x["L0_cond2_Wh"]
    q = np.arange(128) % TB
    cols = np.arange(4 * TOK) // TOK
    arrays = {
        "xT": x["x"].transpose(2, 1, 0).reshape(D, T * B),
        "h0T": x["cond_1024"].T,
        "lWx": x["L0_cond_Wx"].reshape(D, 4, 128),
        "lWh": x["L0_cond_Wh"].reshape(D, 4, 128),
        "bias": np.concatenate([
            x["L0_cond_b"].reshape(4, 1, 128),
            np.stack([x["L0_cond2_br"], x["L0_cond2_bz"], x["L0_cond2_bh"], x["L0_cond2_bp"]]).reshape(4, 1, 128)], axis=1),
        "b1": x["L0_ffn_b1"].reshape(E, FC, 128).transpose(2, 0, 1),
        "b2": x["L0_ffn_b2"],
        "WqT": wq.transpose(2, 1, 0),
        "WkT": x["L0_attn_Wk_up"].transpose(2, 1, 0),
        "WvT": x["L0_attn_Wv_up"].transpose(2, 1, 0),
        "Wout": x["L0_attn_Wout"].transpose(1, 0, 2),
        "Wkvd": x["L0_attn_Wkv_down"],
        "gWx": np.stack([gr[:D], gz[:D], gh[:D]], axis=1),
        "gWh": np.stack([gr[D:], gz[D:], gh[D:]], axis=1),
        "gWp": x["L0_cond2_Wp"],
        "gateW": x["L0_ffn_gate_w"].T,
        "w1": x["L0_ffn_w1"].transpose(1, 0, 2),
        "w2": x["L0_ffn_w2"].reshape(E, FC, 128, D).transpose(2, 0, 1, 3),
        "ident": np.eye(128, dtype=np.float32),
        "ind": (np.arange(12)[:, None] % 4 == cols[None, :]).astype(np.float32),
        "gscale": np.array([[0.5, 0.5], [0.5, 0.5], [0.5, 1.0], [1.0, 1.0]], np.float32) * np.float32(SP),
        "mask": np.where(np.arange(TB)[None, :] > q[:, None], np.float32(NEG), np.float32(0)),
        "tri": np.broadcast_to(np.tril(np.ones((E, E), np.float32), -1), (128, E, E)),
    }
    nc = _bacc.Bacc("TRN2", target_bir_lowering=False, num_devices=1)
    given, aps = {}, {}
    for name, v in arrays.items():
        v = np.ascontiguousarray(v)
        given[f"in_{name}"] = v
        aps[name] = nc.dram_tensor(f"in_{name}", v.shape, mybir.dt.from_np(v.dtype), kind="ExternalInput").ap()
    out = nc.dram_tensor("out", ((NG + 2) * TOK, D), mybir.dt.float32, kind="ExternalOutput").ap()
    build(nc, aps, out)
    r = _run(nc, [given], core_ids=[0])
    got = r.results[0]["out"]
    return got[2 * TOK:].reshape(T, B, D).transpose(1, 0, 2)
```

```python
import numpy as np
import concourse.bass as bass
from concourse import mybir
from contextlib import ExitStack

B, T, D = 16, 128, 128
H, HD, LD = 16, 64, 32
E, F = 8, 512
GS = 8
TOK = GS * B
NG = T // GS
TB = 32
NBLK = T // TB
HQ = 128 // TB
HG = H // HQ
BQ = B // (TB // GS)
PAD = T * B
FC = F // 128
NEG = -1.0e30
SH = 256.0
SW = 256.0
SP = SH * SW


def build(nc, a, out):
    f32 = mybir.dt.float32
    f16 = mybir.dt.float16
    bf16 = mybir.dt.bfloat16
    ALU = mybir.AluOpType
    ACT = mybir.ActivationFunctionType
    AX = mybir.AxisListType
    ds = bass.ds

    ctx = ExitStack()
    with ctx:
        def sb(name, shape, dt=f32):
            return ctx.enter_context(nc.sbuf_tensor(name, shape, dt))

        def pb(name, shape, dt=f32):
            return ctx.enter_context(nc.psum_tensor(name, shape, dt))

        def sem(name):
            return ctx.enter_context(nc.semaphore(name))

        ident = sb("ident", [128, 128])
        ident16 = sb("ident16", [128, 128], bf16)
        ind32 = sb("ind32", [12, 4 * TOK])
        ind = sb("ind", [12, 4 * TOK], bf16)
        gscale = sb("gscale", [4, 2])
        mask32 = sb("mask32", [128, TB])
        cmask = sb("cmask", [128, HG, TB], bf16)
        xT = sb("xT", [128, PAD + TB * B + B])
        h0T = sb("h0T", [128, B])
        lWx = sb("lWx", [128, 4, 128])
        lWh = sb("lWh", [128, 4, 128])
        bias = sb("bias", [4, 2, 128])
        bres = sb("bres", [4, 2, 128])
        bpart = [sb(f"bpart{n}", [4, 2, 128], bf16) for n in range(3)]
        biasP = sb("biasP", [12, 2, 128], bf16)
        b1 = sb("b1", [128, E, FC])
        b2 = sb("b2", [E, D])
        b2res = sb("b2res", [E, D])
        b2part = [sb(f"b2part{n}", [E, D], bf16) for n in range(3)]
        b2P = sb("b2P", [3, E * D], bf16)
        ones3 = sb("ones3", [3, 128], bf16)
        WqT = sb("WqT", [HD, H, D])
        WkT = sb("WkT", [HD, H, LD])
        WvT = sb("WvT", [HD, H, LD])
        Wout = sb("Wout", [HD, H, D])
        Wkvd = sb("Wkvd", [128, HQ, LD])
        Wqk = sb("Wqk", [128, H, LD])
        Wqkhi = sb("Wqkhi", [128, H, LD], f16)
        Wqklo = sb("Wqklo", [128, H, LD], f16)
        Wkvdhi = sb("Wkvdhi", [128, HQ, LD], f16)
        Wkvdlo = sb("Wkvdlo", [128, HQ, LD], f16)
        Wvo = sb("Wvo", [128, HG, D])
        gWx = sb("gWx", [128, 3, 128])
        gWh = sb("gWh", [128, 3, 128])
        gW1 = sb("gW1", [128, 3, 128])
        gW2 = sb("gW2", [128, 3, 128])
        gWhi = sb("gWhi", [128, 2, 128], f16)
        gWlo = sb("gWlo", [128, 2, 128], f16)
        lWhi = sb("lWhi", [128, 4, 128], f16)
        lWlo = sb("lWlo", [128, 4, 128], f16)
        w1hi = sb("w1hi", [128, E, F], f16)
        w1lo = sb("w1lo", [128, E, F], f16)
        gWp = sb("gWp", [128, 128])
        gateW = sb("gateW", [128, E])
        w1 = sb("w1", [128, E, F])
        w2 = sb("w2", [128, E, FC, D])

        hfull = sb("hfull", [128, B])
        still = sb("still", [128, 512], bf16)
        hhi = sb("hhi", [128, 2 * GS, B], f16)
        hlo = sb("hlo", [128, 2 * GS, B], f16)
        oK = sb("oK", [128, B])
        lT = sb("lT", [128, 5, B])
        lP = sb("lP", [128, 2, B])
        lC = sb("lC", [128, B])
        latT = sb("latT", [128, B, GS + T])
        latS = sb("latS", [128, BQ, TB])
        latR = sb("latR", [128, BQ, LD])
        latN = sb("latN", [128, B, LD + 1])
        qT = sb("qT", [128, 2, HG, B, TB])
        qbd = sb("qbd", [128, 2, HG, HQ, TB])
        mx = sb("mx", [128, 2, HG])
        P = sb("P", [128, BQ, HG, T])
        PTs = sb("PTs", [128, 2, HG, 128])
        rs = sb("rs", [128, HG])
        On = sb("On", [128, HG, LD])
        OT = sb("OT", [128, HG, BQ, TB])
        x1T = sb("x1T", [128, TOK + PAD + TB * B + B])
        g8 = sb("g8", [128, 2 * GS + 2, B])
        gp = g8[:, 2 * GS, :]
        ghi = sb("ghi", [128, 2 * GS, B], f16)
        glo = sb("glo", [128, 2 * GS, B], f16)
        gT = sb("gT", [128, 2, B])
        gRZ = sb("gRZ", [128, 2, B])
        gA = sb("gA", [128, B])
        gC = sb("gC", [128, B])
        gB = sb("gB", [128, B])
        tri = sb("tri", [128, E, E])
        stx = sb("stx", [128, TOK])
        xn = sb("xn", [128, D])
        hidA = sb("hidA", [128, 2, TOK])
        hidB = sb("hidB", [128, 2, TOK])
        lg = sb("lg", [128, E])
        lmax = sb("lmax", [128, 1])
        low = sb("low", [128, E])
        th = sb("th", [128, E])
        eq = sb("eq", [128, E, E])
        gt = sb("gt", [128, E, E])
        rank = sb("rank", [128, E])
        den = sb("den", [128, E])
        ex = sb("ex", [128, E])
        picked = sb("picked", [128, E])
        sums = sb("sums", [128, 4])
        gates = sb("gates", [128, 2, E])
        acc = sb("acc", [128, 2, D])

        pL = [pb(f"pL{n}", [128, 4, GS, B]) for n in range(2)]
        p2 = pb("p2", [128, 512])
        p3 = pb("p3", [128, 512])
        p4 = pb("p4", [128, 512])
        p5 = pb("p5", [128, 512])
        p6 = pb("p6", [128, 512])
        p7 = pb("p7", [128, 512])
        pS = [p2, p3]
        pT, pQ, pO, pM = p4, p5, p6, p7
        pX = pL[1][:, :, :, :].rearrange("p g s b -> p (g s b)")
        pG = pL
        pHA, pHB, pY, pR = p2, p3, [p4, p5], p6

        loaded = sem("loaded")
        loaded2 = sem("loaded2")
        loaded3 = sem("loaded3")
        loaded_x = sem("loaded_x")
        loaded_bias = sem("loaded_bias")
        loaded_fold = sem("loaded_fold")
        stacked2 = sem("stacked2")
        set_gru = sem("set_gru")
        set_still = sem("set_still")
        set_pool = sem("set_pool")
        set_dve = sem("set_dve")
        set_act = sem("set_act")
        fold_mm = sem("fold_mm")
        folded = sem("folded")
        split = sem("split")
        stacked = sem("stacked")
        opened = sem("opened")
        l_gates = sem("l_gates")
        l_tanh = sem("l_tanh")
        l_mul = sem("l_mul")
        l_c = sem("l_c")
        l_tc = sem("l_tc")
        l_h = sem("l_h")
        l_hi = sem("l_hi")
        l_lo = sem("l_lo")
        g_hi = sem("g_hi")
        g_lo = sem("g_lo")
        w1_split = sem("w1_split")
        lat_mm = sem("lat_mm")
        q_mm = sem("q_mm")
        lat_done = sem("lat_done")
        q_done = sem("q_done")
        lat_staged = sem("lat_staged")
        lat_turned = sem("lat_turned")
        latn_done = sem("latn_done")
        qbd_done = sem("qbd_done")
        qbd_last = sem("qbd_last")
        qbd_first = sem("qbd_first")
        s_mm = sem("s_mm")
        mx_done = sem("mx_done")
        sub_done = sem("sub_done")
        exp_done = sem("exp_done")
        pt_mm = sem("pt_mm")
        pt_done = sem("pt_done")
        o_mm = sem("o_mm")
        rs_done = sem("rs_done")
        on_done = sem("on_done")
        ot_done = sem("ot_done")
        proj_mm = sem("proj_mm")
        x1_done = sem("x1_done")
        g_rz = sem("g_rz")
        g_tanh = sem("g_tanh")
        g_rh = sem("g_rh")
        g_a = sem("g_a")
        g_cand = sem("g_cand")
        g_c = sem("g_c")
        g_b = sem("g_b")
        g_h = sem("g_h")
        g_prop = sem("g_prop")
        g_p = sem("g_p")
        stx_done = sem("stx_done")
        r_mm = sem("r_mm")
        route = sem("route")
        th_done = sem("th_done")
        l1a = sem("l1a")
        l1b = sem("l1b")
        gelu_a = sem("gelu_a")
        gelu_b = sem("gelu_b")
        l2a = sem("l2a")
        l2b = sem("l2b")
        acc_done = sem("acc_done")
        stored = [sem(f"stored{n}") for n in range(2)]

        block = ctx.enter_context(nc.Block())

        def whole(t):
            return t[tuple(slice(None) for _ in t.shape)]

        LOADS = [(lWh, "lWh"), (h0T, "h0T"), (lWx, "lWx"), (ident, "ident"), (ind32, "ind")]
        FOLDED = [(WqT, "WqT"), (WkT, "WkT"), (WvT, "WvT"), (Wout, "Wout")]
        LOADS2 = [(mask32, "mask"), (b2, "b2")]
        LOADS3 = [(gWx, "gWx"), (gWh, "gWh"), (gWp, "gWp"), (gateW, "gateW"), (tri, "tri"), (b1, "b1"), (w1, "w1"), (w2, "w2")]
        N1 = 16 * len(LOADS)
        N2 = 16 * (len(LOADS2) + HQ)
        N3 = 16 * len(LOADS3)
        CLEARED = [P, lT, qbd, latN, OT, stx, hidA, hidB, ghi, glo, acc, gates]
        NSET = len(CLEARED) + 7
        LAST = BQ * 4 * (NBLK - 1)
        POOLED = HQ * BQ - 2
        AGAIN = 128 // (LD + 1)
        SETG = 7
        SETL = 2 + 4 + 4
        SETD = SETL + 4 + 1
        SETA = 14
        VALUES = [(), (), (), (), (), (0,), (1,), (2, 3)]
        ROUTE = 18

        def V_of(k):
            return (pO, pM)[k % 2][:, 0:HG * AGAIN * (LD + 1)].rearrange("p (g r c) -> p g r c", g=HG, r=AGAIN)

        def O_of(k):
            return V_of(k)[:, :, 0, :]

        @block.sync
        def _(sp):
            sp.sem_inc(stored[0], 16)
            sp.dma_start(whole(bias), a["bias"]).then_inc(loaded_bias, 16)
            sp.dma_start(whole(gscale), a["gscale"]).then_inc(loaded_bias, 16)
            for t, name in LOADS:
                sp.dma_start(whole(t), a[name]).then_inc(loaded, 16)
            sp.wait_ge(split, 1)
            for n in range(3):
                sp.dma_start(biasP[4 * n:4 * n + 4, :, :], whole(bpart[n])).then_inc(stacked, 16)
            for q in range(HQ):
                sp.dma_start(Wkvd[:, q, :], a["Wkvd"]).then_inc(loaded2, 16)
            for t, name in LOADS3[:-2]:
                sp.dma_start(whole(t), a[name]).then_inc(loaded3, 16)
            sp.wait_ge(split, 2)
            for n in range(3):
                sp.dma_start(b2P[n:n + 1, :], whole(b2part[n])).then_inc(stacked2, 16)
            for t, name in LOADS3[-2:]:
                sp.dma_start(whole(t), a[name]).then_inc(loaded3, 16)
            with sp.Fori(0, NG // 2) as i:
                for hf in range(2):
                    sp.wait_ge(acc_done, 16 * i + (8 * hf + 5) + 1)
                    sp.dma_start(out[ds(i * (2 * TOK) + hf * TOK, TOK), :], acc[:, 1 - hf, :]).then_inc(stored[1 - hf], 16)
            for hf in range(2):
                sp.wait_ge(acc_done, 8 * (NG + hf) + 5 + 1)
                sp.dma_start(out[(NG + hf) * TOK:(NG + hf + 1) * TOK, :], acc[:, 1 - hf, :]).then_inc(stored[1 - hf], 16)
            for n in range(2):
                sp.wait_ge(stored[n], 16 * (NG // 2 + 2 - n))

        @block.gpsimd
        def _(pool):
            pool.sem_inc(latn_done, 1)
            for t in CLEARED:
                pool.memset(whole(t), 0.0).then_inc(set_pool, 1)
            pool.memset(xT[:, PAD:], 0.0).then_inc(set_pool, 1)
            pool.memset(x1T[:, 0:TOK], 0.0).then_inc(set_pool, 1)
            pool.memset(x1T[:, TOK + PAD:], 0.0).then_inc(set_pool, 1)
            pool.memset(g8[:, 0:2 * GS, :], 0.0).then_inc(set_pool, 1)
            pool.memset(g8[:, 2 * GS + 1, :], SH / 2).then_inc(set_pool, 1)
            pool.memset(whole(ones3), 1.0).then_inc(set_pool, 1)
            pool.wait_ge(set_pool, NSET - 1)
            pool.memset(latN[:, :, LD:LD + 1], 1.0).then_inc(set_pool, 1)
            pool.wait_ge(loaded3, N3)
            pool.tensor_scalar(whole(w1hi), whole(w1), SW, None, ALU.mult).then_inc(w1_split, 1)
            pool.tensor_scalar(whole(w1), whole(w1), SW, None, ALU.mult).then_inc(w1_split, 1)
            pool.wait_ge(w1_split, 2)
            pool.tensor_tensor(whole(w1lo), whole(w1), whole(w1hi), ALU.subtract).then_inc(w1_split, 1)
            pool.wait_ge(w1_split, 3)
            for j in range(NBLK):
                rows = slice(TB * j, TB * (j + 1))
                with pool.Fori(0, 2) as i:
                    for hf in range(2):
                        turn = 2 * i + (4 * j + hf)
                        b0 = 2 * BQ * i + BQ * hf
                        pool.wait_ge(lat_done, 4 * (j + 1) + 1 + 1)
                        pool.wait_ge(lat_turned, turn + 1)
                        pool.tensor_copy(latS[rows, :, :],
                                         latT[rows, ds(b0, BQ), GS + TB * j:GS + TB * (j + 1)]).then_inc(lat_staged, 1)
                        pool.wait_ge(q_done, 4 * (j + 1) + 1 + 1)
                        for k in range(BQ):
                            if k == 2:
                                pool.wait_ge(lat_turned, turn + 1 + 1)
                                pool.tensor_copy(latN[rows, ds(b0, BQ), 0:LD], latR[rows, :, :]).then_inc(latn_done, 1)
                            pool.wait_ge(s_mm, BQ * turn + (k + 1))
                            for q in range(HQ - 1 if j == NBLK - 1 else HQ - 2 if k == 0 else HQ):
                                r = slice(32 * q, 32 * q + 32)
                                pool.tensor_copy(qbd[r, k % 2, :, q, :], qT[r, j % 2, :, ds(b0 + k, 1), :]
                                                 .rearrange("p g o t -> p g (o t)")).then_inc(qbd_done, 1)

            def stage(G, off):
                pool.wait_ge(r_mm, 2 * G + 1)
                pool.tensor_copy(whole(stx), x1T[:, off]).then_inc(stx_done, 1)

            pool.wait_ge(x1_done, 4 * NBLK + 1)
            with pool.Fori(0, NG // 2) as i:
                for hf in range(2):
                    stage(2 * i + hf, ds(i * (2 * TOK) + hf * TOK, TOK))
            stage(NG, slice(NG * TOK, (NG + 1) * TOK))

        @block.tensor
        def _(pe):
            def mm(out, lhsT, rhs, start=False, stop=True):
                return nc.tensor.matmul(out, lhsT=lhsT, rhs=rhs, start=start, stop=stop, skip_group_check=True)

            def flat(t):
                return t.rearrange("p a b -> p (a b)")

            def keep_warm(n):
                for _ in range(n):
                    mm(pQ[:, :], still[:, 0:128], still[:, :], start=True)

            pe.sem_inc(s_mm, 2)
            pe.sem_inc(pt_mm, BQ)
            for x in (r_mm, l1a, l1b, l2a, l2b):
                pe.sem_inc(x, 1)
            pe.wait_ge(set_still, 3)
            keep_warm(17)
            pe.wait_ge(loaded_fold, 16 * len(FOLDED))
            for h in range(H):
                mm(p2[:, LD * h:LD * (h + 1)], WqT[:, h, :], WkT[:, h, :], start=True)
            for h in range(H):
                q, g = h % HQ, h // HQ
                last = mm(p3[32 * q:32 * q + 32, D * g:D * (g + 1)], WvT[:, h, :], Wout[:, h, :], start=True)
            last.then_inc(fold_mm, 1)
            keep_warm(15)
            pe.wait_ge(set_pool, NSET)
            pe.wait_ge(set_dve, SETL)
            pe.wait_ge(set_act, SETA)
            pe.wait_ge(stacked, 16 * 3)
            pe.wait_ge(loaded_x, 16)

            def l_fill(G, hf, g):
                if g == 0:
                    mm(pL[hf][:, :, :, :].rearrange("p g s b -> p (g s b)"), biasP[:, 0, :], ind[:, :], start=True)
                return mm(pL[hf][:, g, :, :].rearrange("p s b -> p (s b)"), lWx[:, g, :], xT[:, ds(G * TOK, TOK)])

            for g in range(4):
                l_fill(0, 0, g)

            def lat_q(turn, hf, after_values):
                hi, lo = (t[:, GS * (1 - hf):GS * (2 - hf), :].rearrange("p s b -> p (s b)") for t in (hhi, hlo))
                pe.wait_ge(l_lo, GS * turn + 1)
                pe.wait_ge(lat_done, turn + 1)
                pe.wait_ge(q_done, turn + 1)
                if after_values:
                    pe.wait_ge(on_done, BQ * turn - (4 * BQ - 2))
                mm(pM[:, 0:TOK], flat(Wkvdhi[:, :, :]), hi, start=True)
                mm(pM[:, 0:TOK], flat(Wkvdhi[:, :, :]), lo)
                mm(pM[:, 0:TOK], flat(Wkvdlo[:, :, :]), hi).then_inc(lat_mm, 1)
                for g in range(HG):
                    Y, heads = pQ[:, TOK * g:TOK * (g + 1)], slice(HQ * g, HQ * (g + 1))
                    mm(Y, flat(Wqkhi[:, heads, :]), hi, start=True)
                    mm(Y, flat(Wqkhi[:, heads, :]), lo)
                    last = mm(Y, flat(Wqklo[:, heads, :]), hi)
                last.then_inc(q_mm, 1)

            def project(turn, bank=pO):
                pe.wait_ge(ot_done, BQ * turn + 1)
                if bank is pX:
                    pe.wait_ge(x1_done, turn)
                for g in range(HG):
                    last = mm(bank[:, 384:384 + TOK], Wvo[:, g, :], flat(OT[:, g, :, :]), start=(g == 0))
                last.then_inc(proj_mm, 1)

            def scores(n, k, L, b, turn, last_block=False):
                if last_block:
                    pe.wait_ge(qbd_done, 3 * n + (POOLED * 4 * (NBLK - 1) - 3 * LAST + 3))
                    pe.wait_ge(qbd_last, n - (LAST - 1))
                else:
                    pe.wait_ge(qbd_done, POOLED * turn + (HQ * k + HQ - 2))
                    if k == 0:
                        pe.wait_ge(qbd_first, 2 * turn + 2)
                pe.wait_ge(sub_done, n + 1)
                S = pS[k % 2]
                mm(S[:, :].rearrange("p (g t) -> p g t", g=HG)[:, :, L - TB:L], ident16[:, :],
                   cmask[:, :, :], start=True)
                again = T // L
                for g in range(HG):
                    last = mm(S[:, T * g:T * g + again * L].rearrange("p (r t) -> p r t", r=again), flat(qbd[:, k % 2, g, :, :]),
                              latT[:, ds(b, 1), GS:GS + L].to_broadcast([128, again, L]))
                last.then_inc(s_mm, 1)

            def turn_probs(n, k, L):
                pe.wait_ge(exp_done, n + 1)
                pe.wait_ge(pt_done, n + 1)
                for g in range(HG):
                    last = nc.tensor.transpose(pT[:, 128 * g:128 * (g + 1)], P[:, k, g, :], ident[:, :])
                last.then_inc(pt_mm, 1)

            def values(n, k, L, b, turn, last_block=False):
                pe.wait_ge(pt_done, n + 1 + 1)
                if k == 0:
                    pe.wait_ge(latn_done, turn + 1 + 1)
                    if not last_block:
                        pe.wait_ge(x1_done, turn + 1)
                pe.wait_ge(on_done, n + 1)
                for g in range(HG):
                    last = mm(V_of(k)[:, g, :, :], PTs[0:L, k % 2, g, :],
                              latN[0:L, ds(b, 1), :].to_broadcast([L, AGAIN, LD + 1]), start=(g == 0))
                last.then_inc(o_mm, 1)

            def attention(s, turn, L, b0):
                if s == 1:
                    project(turn)
                for k in VALUES[s]:
                    values(BQ * turn + k, k, L, b0 + k, turn)
                if 3 <= s <= 6:
                    turn_probs(BQ * turn + (s - 3), s - 3, L)
                if 1 <= s <= 4:
                    scores(BQ * turn + (s - 1), s - 1, L, b0 + (s - 1), turn)

            FILLS = (0, 2, 3, 5)
            WARM = [[0, 4, 4, 5, 5, 4, 4, 5], [0, 0, 1, 0, 0, 1, 1, 1], [0, 0, 1, 0, 0, 1, 1, 1], [0, 0, 0, 0, 0, 1, 2, 0]]
            for p in range(NBLK):
                if p == 1:
                    pe.wait_ge(set_dve, SETD)
                with pe.Fori(0, 2) as i:
                    for hf in range(2):
                        G = 2 * i + (4 * p + hf)
                        for s in range(GS):
                            was = (GS * hf + s - 1) % (2 * GS)
                            pe.wait_ge(l_hi, GS * G + (s + 1))
                            for g in range(4):
                                mm(pL[hf][:, g, s, :], lWhi[:, g, :], hhi[:, was, :])
                                mm(pL[hf][:, g, s, :], lWlo[:, g, :], hhi[:, was, :])
                            pe.wait_ge(l_lo, GS * G + (s + 1))
                            for g in range(4):
                                last = mm(pL[hf][:, g, s, :], lWhi[:, g, :], hlo[:, was, :])
                            last.then_inc(l_gates, 1)
                            if s == 0:
                                lat_q(G, hf, p > 0)
                            if p > 0:
                                attention(s, G - 4, TB * p, 2 * BQ * i + BQ * hf)
                            if s in FILLS:
                                l_fill(G + 1, 1 - hf, FILLS.index(s))
                            if s == 1:
                                pe.wait_ge(lat_done, G + 2)
                                pe.wait_ge(q_done, G + 2)
                            if s > 0:
                                keep_warm(WARM[p][s])

            def g_fill(G, hf, g):
                if g == 0:
                    mm(pG[hf][:, :, :, :].rearrange("p g s b -> p (g s b)"), biasP[:, 1, :], ind[:, :], start=True)
                return mm(pG[hf][:, g, :, :].rearrange("p s b -> p (s b)"), gWx[:, g, :], x1T[:, ds(G * TOK + TOK, TOK)])

            def last_attention(i, first, slots=BQ):
                for k in range(slots):
                    n = 4 * i + (LAST + k)
                    if slots == BQ:
                        scores(n, k, T, 4 * i + k, None, True)
                    else:
                        k += BQ
                    if slots < BQ and k == BQ or slots == BQ and not (first and k == 0):
                        turn_probs(n - 1, (k - 1) % BQ, T)
                    if slots == BQ and k == 2:
                        project(i + 4 * (NBLK - 1), pX)
                    if not (first and k < 2):
                        values(n - 2, (k - 2) % BQ, T, 4 * i + (k % BQ if slots < BQ else k) - 2, i + 4 * (NBLK - 1), True)

            lat_q(4 * NBLK, 0, True)
            pe.wait_ge(lat_done, 4 * NBLK + 1 + 1)
            pe.wait_ge(q_done, 4 * NBLK + 1 + 1)
            keep_warm(6)
            last_attention(0, True)
            with pe.Fori(1, 4) as i:
                last_attention(i, False)
            pe.wait_ge(set_gru, SETG + 1)
            for g in range(3):
                g_fill(0, 0, g)
            last_attention(4, False, 2)
            keep_warm(3)
            pe.wait_ge(stacked2, 16 * 3)
            mm(pY[1][:, :], ones3[:, :], b2P[:, 512:1024], start=True)
            mm(pHB[:, 0:2 * TOK], biasP[:, 1, :], ind[:, 0:2 * TOK], start=True).then_inc(opened, 1)
            project(4 * NBLK, pX)

            pe.wait_ge(x1_done, 4 * NBLK + 1)
            pe.wait_ge(w1_split, 3)

            def route_x(G, hf):
                pe.wait_ge(route, ROUTE * G + 1)
                pe.wait_ge(stx_done, G + 1)
                mm(pR[:, 0:E], g8[:, GS * (1 - hf):GS * (2 - hf), :].rearrange("p s b -> p (s b)"), gateW[:, :],
                   start=True).then_inc(r_mm, 1)
                nc.tensor.transpose(pR[:, 128:256], stx[:, :], ident[:, :]).then_inc(r_mm, 1)

            def layer1(G, hf, e, half):
                bank, free, done = ((pHA, gelu_a, l1a), (pHB, gelu_b, l1b))[half]
                pe.wait_ge(free, E * G + (e + half) + 1)
                hi, lo = (t[:, GS * (1 - hf):GS * (2 - hf), :].rearrange("p s b -> p (s b)") for t in (ghi, glo))
                for c in range(2):
                    Y, cols = bank[:, TOK * c:TOK * (c + 1)], slice(128 * (2 * half + c), 128 * (2 * half + c + 1))
                    mm(Y, w1hi[:, e, cols], hi, start=(c == 0))
                    mm(Y, w1hi[:, e, cols], lo)
                    last = mm(Y, w1lo[:, e, cols], hi)
                last.then_inc(done, 1)

            def layer2(G, e, half, chunks=(0, 1)):
                hid, ready, done = ((hidA, gelu_a, l2a), (hidB, gelu_b, l2b))[half]
                Y = pY[e // 4]
                if half == 0 and e % 4 == 0 and 0 in chunks:
                    pe.wait_ge(acc_done, 8 * G + (e + 1) + 1)
                    mm(Y[:, :], ones3[:, :], b2P[:, 512 * (e // 4):512 * (e // 4) + 512], start=True)
                if 0 in chunks:
                    pe.wait_ge(ready, E * G + ((e + 1) % E + half) + 1)
                for c in chunks:
                    last = mm(Y[:, D * (e % 4):D * (e % 4 + 1)], hid[:, c, :], w2[:, e, 2 * half + c, :])
                if c == 1:
                    last.then_inc(done, 1)

            def gru_turn(i, hf, gru, experts, steps=GS):
                G = 2 * i + hf
                for s in range(steps):
                    if gru:
                        if s % 4 == 0:
                            pe.wait_ge(g_p, 2 * G + (s // 4 + 1))
                            W = gW1
                            for g in range(2):
                                last = mm(pG[hf][:, g, s, :], W[:, g, :], gp)
                        else:
                            W = gW2
                            pe.wait_ge(g_hi, GS * G + s)
                            for g in range(2):
                                mm(pG[hf][:, g, s, :], gWhi[:, g, :], ghi[:, GS * hf + s - 1, :])
                                mm(pG[hf][:, g, s, :], gWlo[:, g, :], ghi[:, GS * hf + s - 1, :])
                            pe.wait_ge(g_lo, GS * G + (s + 1))
                            for g in range(2):
                                last = mm(pG[hf][:, g, s, :], gWhi[:, g, :], glo[:, GS * hf + s - 1, :])
                        last.then_inc(g_rz, 1)
                    if experts and s == 0:
                        pe.wait_ge(g_lo, GS * G + 1)
                    if experts:
                        layer1(G, hf, s, 0)
                    layer2(G, (s - 1) % E, 0, (0,))
                    if gru:
                        pe.wait_ge(g_rh, GS * G + (s + 1))
                        mm(pG[hf][:, 2, s, :], W[:, 2, :], gRZ[:, 0, :]).then_inc(g_cand, 1)
                    if s == 0 and experts:
                        route_x(G, hf)
                    layer2(G, (s - 1) % E, 0, (1,))
                    if experts:
                        layer1(G, hf, s, 1)
                    if gru and s % 4 == 3:
                        for g in ((0,), (1, 2))[s // 4]:
                            g_fill(G + 1, 1 - hf, g)
                        pe.wait_ge(g_h, GS * G + (s + 1))
                        mm(pG[hf][:, 3, s, :], gWp[:, :], g8[:, GS * hf + s, :]).then_inc(g_prop, 1)
                    layer2(G, (s - 1) % E, 1)

            with pe.Fori(0, NG // 2) as i:
                for hf in range(2):
                    gru_turn(i, hf, True, True)
            gru_turn(NG // 2, 0, False, True)
            gru_turn(NG // 2, 1, False, False, 1)

        @block.scalar
        def _(act):
            A = nc.scalar.activation
            for t, name in FOLDED:
                act.dma_start(whole(t), a[name]).then_inc(loaded_fold, 16)
            act.dma_start(xT[:, 0:PAD], a["xT"]).then_inc(loaded_x, 16)
            for t, name in LOADS2:
                act.dma_start(whole(t), a[name]).then_inc(loaded2, 16)
            for x in (q_done, pt_done, gelu_a, gelu_b):
                act.sem_inc(x, 1)
            act.wait_ge(loaded, N1)
            A(lWh[:, 0:3, :], lWh[:, 0:3, :], ACT.Copy, scale=0.5 * SW).then_inc(set_act, 1)
            A(lWh[:, 3, :], lWh[:, 3, :], ACT.Copy, scale=SW).then_inc(set_act, 1)
            A(hfull[:, :], h0T[:, :], ACT.Copy, scale=SH).then_inc(set_act, 1)
            A(hhi[:, 2 * GS - 1, :], h0T[:, :], ACT.Copy, scale=SH).then_inc(set_act, 1)
            act.wait_ge(set_act, 4)
            A(lWhi[:, :, :], lWh[:, :, :], ACT.Copy).then_inc(set_act, 1)
            A(lWx[:, 0:3, :], lWx[:, 0:3, :], ACT.Copy, scale=0.5 * SP).then_inc(set_act, 1)
            A(lWx[:, 3, :], lWx[:, 3, :], ACT.Copy, scale=SP).then_inc(set_act, 1)
            A(ind[:, :], ind32[:, :], ACT.Copy).then_inc(set_act, 1)
            act.wait_ge(fold_mm, 1)
            A(Wqk[:, :, :].rearrange("p h c -> p (h c)"), p2[:, :], ACT.Copy, scale=SW / HD ** 0.5).then_inc(set_act, 1)
            A(Wqkhi[:, :, :].rearrange("p h c -> p (h c)"), p2[:, :], ACT.Copy, scale=SW / HD ** 0.5).then_inc(set_act, 1)
            A(Wvo[:, :, :].rearrange("p g d -> p (g d)"), p3[:, :], ACT.Copy).then_inc(set_act, 1)
            act.wait_ge(loaded2, N2)
            A(Wkvdhi[:, :, :], Wkvd[:, :, :], ACT.Copy, scale=SW).then_inc(set_act, 1)
            A(Wkvd[:, :, :], Wkvd[:, :, :], ACT.Copy, scale=SW).then_inc(set_act, 1)
            A(ident16[:, :], ident[:, :], ACT.Copy).then_inc(set_act, 1)

            def q_copy(turn, par, t0):
                act.wait_ge(q_mm, turn + 1)
                A(qT[:, ds(par, 1), :, :, ds(t0, GS)].rearrange("p o g b t -> p (o g) b t"), pQ[:, :].rearrange("p (g s b) -> p g b s", g=HG, b=B),
                  ACT.Copy, scale=1.0 / SP).then_inc(q_done, 1)

            def exps(n, k, L):
                act.wait_ge(sub_done, n + 3)
                A(P[:, k, :, 0:L], P[:, k, :, 0:L], ACT.Exp).then_inc(exp_done, 1)

            def pt_copy(n, k, L):
                act.wait_ge(pt_mm, n + (BQ + 1))
                A(PTs[0:L, k % 2, :, :].rearrange("p g q -> p (g q)"), pT[0:L, :], ACT.Copy).then_inc(pt_done, 1)

            def last_query(n, k, b):
                act.wait_ge(s_mm, n + 1)
                r = slice(128 - 32, 128)
                A(qbd[r, k % 2, :, HQ - 1, :], qT[r, (NBLK - 1) % 2, :, ds(b, 1), :]
                  .rearrange("p g o t -> p g (o t)"), ACT.Copy).then_inc(qbd_last, 1)

            def first_queries(G, turn, b, par):
                act.wait_ge(q_done, G + 2)
                act.wait_ge(s_mm, BQ * turn + 1)
                for q in (HQ - 2, HQ - 1):
                    r = slice(32 * q, 32 * q + 32)
                    A(qbd[r, 0, :, q, :], qT[r, par, :, ds(b, 1), :].rearrange("p g o t -> p g (o t)"),
                      ACT.Copy).then_inc(qbd_first, 1)

            def gru_weights(k):
                if k == 0:
                    act.wait_ge(loaded3, N3)
                    A(gW1[:, :, :], gWh[:, :, :], ACT.Copy, scale=0.5 * SP).then_inc(set_gru, 1)
                if k == 1:
                    A(gW2[:, :, :], gWh[:, :, :], ACT.Copy, scale=0.5 * SW).then_inc(set_gru, 1)
                    A(gWhi[:, :, :], gWh[:, 0:2, :], ACT.Copy, scale=0.5 * SW).then_inc(set_gru, 1)
                if k == 2:
                    A(gWx[:, 0:2, :], gWx[:, 0:2, :], ACT.Copy, scale=0.5 * SP).then_inc(set_gru, 1)
                    A(gWx[:, 2, :], gWx[:, 2, :], ACT.Copy, scale=SP).then_inc(set_gru, 1)
                if k == 3:
                    A(gWp[:, :], gWp[:, :], ACT.Copy, scale=SW).then_inc(set_gru, 1)
                    A(gateW[:, :], gateW[:, :], ACT.Copy, scale=1.0 / SH).then_inc(set_gru, 1)
                    A(gp, h0T[:, :], ACT.Copy).then_inc(g_p, 1)

            def last_attention(i, first, last):
                for k in range(BQ):
                    n = 4 * i + (LAST + k)
                    if first:
                        gru_weights(k)
                    if not (first and k == 0):
                        exps(n - 1, (k - 1) % BQ, T)
                    if not (last and k == BQ - 1):
                        last_query(n + 1, k + 1, 4 * i + k + 1)
                    if not (first and k == 0):
                        pt_copy(n - 1, (k - 1) % BQ, T)

            for p in range(NBLK):
                with act.Fori(0, 2) as i:
                    for hf in range(2):
                        G = 2 * i + (4 * p + hf)
                        turn = 2 * i + (4 * p + hf - 4)
                        for s in range(GS):
                            act.wait_ge(l_gates, GS * G + (s + 1))
                            A(lT[:, 0:4, :], pL[hf][:, :, s, :], ACT.Tanh, scale=1.0 / SP).then_inc(l_tanh, 1)
                            if p > 0 and s == 1:
                                first_queries(G, turn, 2 * BQ * i + BQ * hf, (p - 1) % 2)
                            act.wait_ge(l_c, GS * G + (s + 1))
                            A(lC[:, :], lT[:, 4, :], ACT.Tanh, scale=0.5).then_inc(l_tc, 1)
                            if s == 0 and hf == 0:
                                was, now = (p - 1) % 2, p % 2
                                q_copy(G, i * (now - was) + was, i * (GS - (TB - GS)) + (TB - GS))
                            if s == 0 and hf == 1:
                                q_copy(G, p % 2, 2 * GS * i)
                            if p > 0:
                                L = TB * p
                                if 3 <= s <= 6:
                                    pt_copy(BQ * turn + (s - 3), s - 3, L)
                                if 2 <= s <= 5:
                                    exps(BQ * turn + (s - 2), s - 2, L)
            q_copy(4 * NBLK, (NBLK - 1) % 2, TB - GS)
            act.wait_ge(q_done, 4 * NBLK + 1 + 1)
            last_query(LAST, 0, 0)
            last_attention(0, True, False)
            with act.Fori(1, 3) as i:
                last_attention(i, False, False)
            last_attention(3, False, True)
            exps(LAST + B - 1, BQ - 1, T)
            pt_copy(LAST + B - 1, BQ - 1, T)
            def gelu(n, e, half, step):
                bank, hid, full, read, done = ((pHA, hidA, l1a, l2a, gelu_a), (pHB, hidB, l1b, l2b, gelu_b))[half]
                act.wait_ge(full, n + 1)
                act.wait_ge(read, step + 1)
                for c in range(2):
                    last = A(hid[:, c, :], bank[:, TOK * c:TOK * (c + 1)], ACT.Gelu,
                             bias=b1[:, e, 2 * half + c:2 * half + c + 1], scale=1.0 / SP)
                last.then_inc(done, 1)

            def gru_turn(i, hf, gru, experts, steps=GS):
                G = 2 * i + hf
                for s in range(steps):
                    if gru:
                        act.wait_ge(g_rz, GS * G + (s + 1))
                        A(gT[:, :, :], pG[hf][:, 0:2, s, :], ACT.Tanh, scale=1.0 / SP).then_inc(g_tanh, 1)
                    gelu(E * G + s, (s - 1) % E, 1, E * G + s)
                    if s == 2 and experts:
                        act.wait_ge(route, ROUTE * G + 4 + 1)
                        A(th[:, :], low[:, :], ACT.Tanh, scale=0.5).then_inc(th_done, 1)
                    if gru:
                        act.wait_ge(g_cand, GS * G + (s + 1))
                        A(gC[:, :], pG[hf][:, 2, s, :], ACT.Tanh, scale=1.0 / SP).then_inc(g_c, 1)
                    if experts:
                        gelu(E * G + (s + 1), s, 0, E * G + (s + 1))
                    if gru and s % 4 == 3:
                        act.wait_ge(g_prop, 2 * G + (s // 4 + 1))
                        A(gp, pG[hf][:, 3, s, :], ACT.Tanh, scale=1.0 / SP).then_inc(g_p, 1)

            A(th[:, :], still[:, 0:E], ACT.Gelu)
            act.wait_ge(opened, 1)
            with act.Fori(0, NG // 2) as i:
                for hf in range(2):
                    gru_turn(i, hf, True, True)
            gru_turn(NG // 2, 0, False, True)
            gru_turn(NG // 2, 1, False, False, 1)

        @block.vector
        def _(dve):
            V = nc.vector
            dve.sem_inc(sub_done, 2)
            dve.sem_inc(on_done, 2)
            for x in (lat_turned, lat_done, ot_done, acc_done, route):
                dve.sem_inc(x, 1)
            steps = [0]

            def link(ins):
                steps[0] += 1
                ins.then_inc(set_dve, 1)
                dve.wait_ge(set_dve, steps[0])

            def split3(x, res, parts):
                link(V.tensor_copy(whole(parts[0]), whole(x)))
                link(V.tensor_tensor(whole(res), whole(x), whole(parts[0]), ALU.subtract))
                link(V.tensor_copy(whole(parts[1]), whole(res)))
                link(V.tensor_tensor(whole(res), whole(res), whole(parts[1]), ALU.subtract))
                V.tensor_copy(whole(parts[2]), whole(res)).then_inc(split, 1)

            V.memset(whole(still), 0.0).then_inc(set_still, 1)
            V.memset(hhi[:, 0:2 * GS - 1, :], 0.0).then_inc(set_still, 1)
            V.memset(hlo[:, 0:2 * GS - 1, :], 0.0).then_inc(set_still, 1)
            dve.wait_ge(loaded_bias, 2 * 16)
            for n in range(2):
                link(V.tensor_scalar(bias[:, n, :], bias[:, n, :], gscale[:, n:n + 1], None, ALU.mult))
            split3(bias, bres, bpart)
            dve.wait_ge(set_act, 5)
            link(V.tensor_tensor(lWlo[:, :, :], lWh[:, :, :], lWhi[:, :, :], ALU.subtract))
            link(V.tensor_tensor(hlo[:, 2 * GS - 1, :], hfull[:, :], hhi[:, 2 * GS - 1, :], ALU.subtract))
            dve.wait_ge(set_act, SETA)
            link(V.tensor_tensor(Wqklo[:, :, :], Wqk[:, :, :], Wqkhi[:, :, :], ALU.subtract))
            link(V.tensor_tensor(Wkvdlo[:, :, :], Wkvd[:, :, :], Wkvdhi[:, :, :], ALU.subtract))
            for x in (l_hi, l_lo, l_h, g_lo):
                dve.sem_inc(x, 1)
            dve.wait_ge(loaded2, N2)
            split3(b2, b2res, b2part)
            link(V.tensor_copy(cmask[:, :, :], mask32[:, :].unsqueeze(1).to_broadcast([128, HG, TB])))
            assert steps[0] == SETD
            dve.wait_ge(set_pool, NSET)

            def lat_copy(n):
                dve.wait_ge(lat_mm, n + 1)
                V.tensor_scalar(latT[:, :, ds(n * GS, GS)],
                                pM[:, 0:TOK].rearrange("p (s b) -> p b s", b=B), 1.0 / SP, None, ALU.mult).then_inc(lat_done, 1)

            def add_x(turn, off, bank=pO):
                dve.wait_ge(proj_mm, turn + 1)
                V.tensor_tensor(x1T[:, ds(off + TOK, TB * B)].rearrange("p (t b) -> p b t", b=B)[:, 0:BQ, :],
                                bank[:, 384:384 + TOK].rearrange("p (b t) -> p b t", b=BQ),
                                xT[:, ds(off, TB * B)].rearrange("p (t b) -> p b t", b=B)[:, 0:BQ, :],
                                ALU.add).then_inc(x1_done, 1)

            def S_of(k, L):
                return pS[k % 2][:, :].rearrange("p (g t) -> p g t", g=HG)[:, :, 0:L]

            def maximum(n, k, L):
                dve.wait_ge(s_mm, n + 3)
                V.tensor_reduce(mx[:, k % 2, :], S_of(k, L), AX.X, ALU.max).then_inc(mx_done, 1)

            def subtract(n, k, L):
                dve.wait_ge(mx_done, n + 1)
                dve.wait_ge(pt_mm, n + 1)
                V.tensor_tensor(P[:, k, :, 0:L], S_of(k, L),
                                mx[:, k % 2, :].unsqueeze(2).to_broadcast([128, HG, L]), ALU.subtract).then_inc(sub_done, 1)

            def normaliser(n, k):
                dve.wait_ge(o_mm, n + 1)
                V.reciprocal(rs[:, :].unsqueeze(2), O_of(k)[:, :, LD:LD + 1]).then_inc(rs_done, 1)

            def normalise(n, k):
                dve.wait_ge(rs_done, n + 1)
                V.tensor_tensor(On[:, :, :], O_of(k)[:, :, 0:LD], rs[:, :].unsqueeze(2).to_broadcast([128, HG, LD]),
                                ALU.mult).then_inc(on_done, 1)

            def turn_values(n, k, turn):
                dve.wait_ge(on_done, n + 2 + 1)
                if k == 0:
                    dve.wait_ge(proj_mm, turn + 1)
                V.transpose(OT[:, :, k, :], On[:, :, :]).then_inc(ot_done, 1)

            def turn_latents(turn, rows):
                dve.wait_ge(lat_staged, turn + 1)
                dve.wait_ge(latn_done, turn + 1)
                V.transpose(latR[rows, :, :], latS[rows, :, :]).then_inc(lat_turned, 1)

            for p in range(NBLK):
                rows = slice(TB * (p - 1), TB * p)
                with dve.Fori(0, 2) as i:
                    for hf in range(2):
                        G = 2 * i + (4 * p + hf)
                        turn = 2 * i + (4 * p + hf - 4)
                        for s in range(GS):
                            slot = GS * hf + s
                            dve.wait_ge(l_tanh, GS * G + (s + 1))
                            V.scalar_tensor_tensor(lP[:, :, :], lT[:, 0:2, :], 1.0, lT[:, 3:5, :], ALU.add, ALU.mult).then_inc(l_mul, 1)
                            V.tensor_scalar(oK[:, :], lT[:, 2, :], SH / 2, SH / 2, ALU.mult, ALU.add)
                            dve.wait_ge(l_mul, GS * G + (s + 1))
                            V.scalar_tensor_tensor(lT[:, 4, :], lP[:, 1, :], 0.5, lP[:, 0, :], ALU.mult, ALU.add).then_inc(l_c, 1)
                            if p > 0 and s == 7:
                                normaliser(BQ * turn + 2, 2)
                            if p > 0 and 2 <= s <= 5:
                                subtract(BQ * turn + (s - 2), s - 2, TB * p)
                            dve.wait_ge(l_tc, GS * G + (s + 1))
                            V.tensor_tensor(hhi[:, slot, :], oK[:, :], lC[:, :], ALU.mult).then_inc(l_hi, 1)
                            V.tensor_tensor(hfull[:, :], oK[:, :], lC[:, :], ALU.mult).then_inc(l_h, 1)
                            dve.wait_ge(l_h, GS * G + (s + 2))
                            V.tensor_tensor(hlo[:, slot, :], hfull[:, :], hhi[:, slot, :], ALU.subtract).then_inc(l_lo, 1)
                            if s == 0:
                                lat_copy(G)
                            if p > 0:
                                L = TB * p
                                if s == 0:
                                    turn_latents(turn, rows)
                                if s == 1:
                                    if hf == 0:
                                        was = TB * B * (p - 2 if p > 1 else NBLK) + 3 * BQ
                                        now = TB * B * (p - 1) + BQ
                                        add_x(turn, i * (now - was) + was)
                                    else:
                                        add_x(turn, i * (2 * BQ) + TB * B * (p - 1))
                                if 1 <= s <= 4:
                                    maximum(BQ * turn + (s - 1), s - 1, L)
                                for k in VALUES[s]:
                                    if k != 2:
                                        normaliser(BQ * turn + k, k)
                                    normalise(BQ * turn + k, k)
                                    turn_values(BQ * turn + k, k, turn)

            def last_attention(i, first, slots=BQ):
                turn = i + 4 * (NBLK - 1)
                off = TB * B * (NBLK - 1)
                for k in range(slots):
                    n = 4 * i + (LAST + k)
                    if slots == BQ and k == 0:
                        turn_latents(turn, slice(TB * (NBLK - 1), TB * NBLK))
                    if slots == BQ and k == 3:
                        add_x(turn, off - TB * B + 3 * BQ if first else 4 * i + (off - BQ), pX)
                    if not (first and k < 3):
                        normaliser(n - 3, (k - 3) % BQ)
                        normalise(n - 3, (k - 3) % BQ)
                        turn_values(n - 3, (k - 3) % BQ, turn)
                    if slots == BQ:
                        maximum(n, k, T)
                        subtract(n, k, T)

            lat_copy(4 * NBLK)
            last_attention(0, True)
            dve.wait_ge(set_gru, SETG)
            V.tensor_tensor(gWlo[:, :, :], gW2[:, 0:2, :], gWhi[:, :, :], ALU.subtract).then_inc(set_gru, 1)
            with dve.Fori(1, 4) as i:
                last_attention(i, False)
            last_attention(4, False, 3)
            add_x(4 * NBLK, TB * B * (NBLK - 1) + 3 * BQ, pX)

            def routing(G, hf, s, late):
                li, lj = lg[:, :].unsqueeze(2).to_broadcast([128, E, E]), lg[:, :].unsqueeze(1).to_broadcast([128, E, E])
                ops = [
                    (0, 1, lambda: V.tensor_copy(lg[:, :], pR[:, 0:E])),
                    (0, 1, lambda: V.tensor_copy(xn[:, :], pR[:, 128:256])),
                    (0, 1, lambda: V.tensor_reduce(lmax[:, :], lg[:, :], AX.X, ALU.max)),
                    (1, 0, lambda: V.tensor_scalar(low[:, :], lg[:, :], lmax[:, 0:1], None, ALU.subtract)),
                    (1, 1, lambda: V.tensor_tensor(eq[:, :, :], lj, li, ALU.is_equal)),
                    (1, 1, lambda: V.tensor_tensor(gt[:, :, :], lj, li, ALU.is_gt)),
                    (2, 0, lambda: V.tensor_tensor(eq[:, :, :], eq[:, :, :], tri[:, :, :], ALU.mult)),
                    (2, 1, lambda: V.tensor_tensor(gt[:, :, :], gt[:, :, :], eq[:, :, :], ALU.add)),
                    (2, 1, lambda: V.tensor_reduce(rank[:, :], gt[:, :, :], AX.X, ALU.add)),
                    (3, 0, lambda: V.tensor_scalar(den[:, :], th[:, :], -1.0, 1.0, ALU.mult, ALU.add)),
                    (3, 1, lambda: V.reciprocal(den[:, :], den[:, :])),
                    (3, 1, lambda: V.scalar_tensor_tensor(ex[:, :], th[:, :], 1.0, den[:, :], ALU.add, ALU.mult)),
                    (4, 0, lambda: V.tensor_reduce(sums[:, 0:1], ex[:, :], AX.X, ALU.add)),
                    (4, 1, lambda: V.scalar_tensor_tensor(picked[:, :], rank[:, :], 2.0, ex[:, :], ALU.is_lt, ALU.mult)),
                    (4, 1, lambda: V.tensor_reduce(sums[:, 1:2], picked[:, :], AX.X, ALU.add)),
                    (4, 1, lambda: V.scalar_tensor_tensor(sums[:, 2:3], sums[:, 0:1], 1.0e-9, sums[:, 1:2], ALU.mult, ALU.add)),
                    (5, 0, lambda: V.reciprocal(sums[:, 3:4], sums[:, 2:3])),
                    (5, 0, lambda: V.tensor_scalar(gates[:, hf, :], picked[:, :], sums[:, 3:4], None, ALU.mult)),
                ]
                assert len(ops) == ROUTE
                for at, (step, when, op) in enumerate(ops):
                    if (step, when) != (s, late):
                        continue
                    if at == 0:
                        dve.wait_ge(r_mm, 2 * G + 2 + 1)
                    if at == 9:
                        dve.wait_ge(th_done, G + 1)
                    dve.wait_ge(route, ROUTE * G + at + 1)
                    op().then_inc(route, 1)

            def combine(i, hf, slot, s):
                G = 2 * i + hf
                e = (s - 5) % E
                Y = pY[e // 4][:, :].rearrange("p (e d) -> p e d", e=4)
                if s in (1, 5):
                    dve.wait_ge(l2b, E * G + {1: 2, 5: 6}[s])
                if s == 5:
                    dve.wait_ge(stored[hf], 16 * i + 16)
                    dve.wait_ge(route, ROUTE * G + ROUTE + 1)
                old = xn[:, :] if e == 0 else acc[:, slot, :]
                dve.wait_ge(acc_done, 8 * G + (s + 1))
                V.scalar_tensor_tensor(acc[:, slot, :], Y[:, e % 4, :], gates[:, slot, e:e + 1], old,
                                       ALU.mult, ALU.add).then_inc(acc_done, 1)

            def gru_turn(i, hf, gru, experts, steps=GS):
                G = 2 * i + hf
                for s in range(steps):
                    if gru:
                        slot = GS * hf + s
                        at = 2 * GS if s % 4 == 0 else slot - 1
                        prev, last = g8[:, at, :], 2 * GS + 1
                        t1 = GS * G + (s + 1)
                        dve.wait_ge(g_tanh, t1)
                        V.scalar_tensor_tensor(gRZ[:, :, :], gT[:, :, :], 1.0, g8[:, at:last + 1:last - at, :],
                                               ALU.add, ALU.mult).then_inc(g_rh, 1)
                        V.scalar_tensor_tensor(gA[:, :], gT[:, 1, :], -1.0, prev, ALU.add, ALU.mult).then_inc(g_a, 1)
                    if experts:
                        routing(G, hf, s, 0)
                    if s < 5:
                        combine(i, hf, 1 - hf, s)
                    elif experts:
                        combine(i, hf, hf, s)
                    if gru:
                        dve.wait_ge(g_c, t1)
                        V.tensor_tensor(gB[:, :], gRZ[:, 1, :], gC[:, :], ALU.mult).then_inc(g_b, 1)
                        dve.wait_ge(g_b, t1)
                        keep = -SH / 2 if s % 4 == 0 else -0.5
                        new = lambda o: V.scalar_tensor_tensor(o, gA[:, :], keep, gB[:, :], ALU.mult, ALU.add)
                        new(ghi[:, slot, :]).then_inc(g_hi, 1)
                        new(g8[:, slot, :]).then_inc(g_h, 1)
                        dve.wait_ge(g_h, t1)
                        V.tensor_tensor(glo[:, slot, :], g8[:, slot, :], ghi[:, slot, :], ALU.subtract).then_inc(g_lo, 1)
                    if experts:
                        routing(G, hf, s, 1)

            with dve.Fori(0, NG // 2) as i:
                for hf in range(2):
                    gru_turn(i, hf, True, True)
            gru_turn(NG // 2, 0, False, True)
            gru_turn(NG // 2, 1, False, False, 5)


def kernel(**inputs):
    import concourse.bacc as _bacc
    from concourse.bass_utils import run_bass_kernel_spmd as _run

    x = {k: np.asarray(v) for k, v in inputs.items()}
    wq = x["L0_attn_Wq"]
    gz, gr, gh = x["L0_cond2_Wz"], x["L0_cond2_Wr"], x["L0_cond2_Wh"]
    q = np.arange(128) % TB
    cols = np.arange(4 * TOK) // TOK
    arrays = {
        "xT": x["x"].transpose(2, 1, 0).reshape(D, T * B),
        "h0T": x["cond_1024"].T,
        "lWx": x["L0_cond_Wx"].reshape(D, 4, 128),
        "lWh": x["L0_cond_Wh"].reshape(D, 4, 128),
        "bias": np.concatenate([
            x["L0_cond_b"].reshape(4, 1, 128),
            np.stack([x["L0_cond2_br"], x["L0_cond2_bz"], x["L0_cond2_bh"], x["L0_cond2_bp"]]).reshape(4, 1, 128)], axis=1),
        "b1": x["L0_ffn_b1"].reshape(E, FC, 128).transpose(2, 0, 1),
        "b2": x["L0_ffn_b2"],
        "WqT": wq.transpose(2, 1, 0),
        "WkT": x["L0_attn_Wk_up"].transpose(2, 1, 0),
        "WvT": x["L0_attn_Wv_up"].transpose(2, 1, 0),
        "Wout": x["L0_attn_Wout"].transpose(1, 0, 2),
        "Wkvd": x["L0_attn_Wkv_down"],
        "gWx": np.stack([gr[:D], gz[:D], gh[:D]], axis=1),
        "gWh": np.stack([gr[D:], gz[D:], gh[D:]], axis=1),
        "gWp": x["L0_cond2_Wp"],
        "gateW": x["L0_ffn_gate_w"].T,
        "w1": x["L0_ffn_w1"].transpose(1, 0, 2),
        "w2": x["L0_ffn_w2"].reshape(E, FC, 128, D).transpose(2, 0, 1, 3),
        "ident": np.eye(128, dtype=np.float32),
        "ind": (np.arange(12)[:, None] % 4 == cols[None, :]).astype(np.float32),
        "gscale": np.array([[0.5, 0.5], [0.5, 0.5], [0.5, 1.0], [1.0, 1.0]], np.float32) * np.float32(SP),
        "mask": np.where(np.arange(TB)[None, :] > q[:, None], np.float32(NEG), np.float32(0)),
        "tri": np.broadcast_to(np.tril(np.ones((E, E), np.float32), -1), (128, E, E)),
    }
    nc = _bacc.Bacc("TRN2", target_bir_lowering=False, num_devices=1)
    given, aps = {}, {}
    for name, v in arrays.items():
        v = np.ascontiguousarray(v)
        given[f"in_{name}"] = v
        aps[name] = nc.dram_tensor(f"in_{name}", v.shape, mybir.dt.from_np(v.dtype), kind="ExternalInput").ap()
    out = nc.dram_tensor("out", ((NG + 2) * TOK, D), mybir.dt.float32, kind="ExternalOutput").ap()
    build(nc, aps, out)
    r = _run(nc, [given], core_ids=[0])
    got = r.results[0]["out"]
    return got[2 * TOK:].reshape(T, B, D).transpose(1, 0, 2)
```
